# Optimizing a Trainium2 kernel written in Bass

```python
import numpy as np
import jax
import jax.numpy as jnp

def _softmax(x, axis=-1):
    return jax.nn.softmax(x, axis=axis)

def _gelu(x):
    return jax.nn.gelu(x, approximate=True)

def _silu(x):
    return jax.nn.silu(x)

def _sigmoid(x):
    return jax.nn.sigmoid(x)

def _layernorm(x, axis=-1, eps=1e-05):
    m = jnp.mean(x, axis=axis, keepdims=True)
    v = jnp.var(x, axis=axis, keepdims=True)
    return (x - m) / jnp.sqrt(v + eps)

def _scatter_add(tgt, idx, src, axis=0):
    return tgt.at[idx].add(src)

def _segment_sum(src, seg, n):
    return jax.ops.segment_sum(src, seg, n)
kernel_name = 'mk_flamingo_gated_d2_seqx_r8_3686c6'

def setup_inputs(seed: int=0):
    np.random.seed(seed)
    _w = jnp.asarray

    def _rec_inputs():
        import jax
        import jax.numpy as jnp
        _rk = jax.random.key(seed)
        x = 6.313e-05 + 0.9998 * jax.random.normal(jax.random.fold_in(_rk, 1), (8, 56, 128), jnp.float32)
        _lenS = 56 - jax.random.randint(jax.random.fold_in(_rk, 7), (8,), 0, max(1, 56 // 4) + 1, jnp.int32)
        _lenS2 = 1500 - jax.random.randint(jax.random.fold_in(_rk, 8), (8,), 0, max(1, 1500 // 4) + 1, jnp.int32)
        _ctx_1024P = jax.random.normal(jax.random.fold_in(_rk, 11), (8, 16, 128), jnp.float32)
        _ctx_1024c = jax.random.dirichlet(jax.random.fold_in(_rk, 511), 0.3 * jnp.ones((16,), jnp.float32), (8, 1500))
        _ctx_1024t = jnp.einsum('bsk,bkd->bsd', _ctx_1024c, _ctx_1024P)
        _ctx_1024t = _ctx_1024t * jax.lax.rsqrt(jnp.mean(jnp.square(_ctx_1024t)) + 1e-12) * 0.953939
        ctx_1024 = -0.000214406 + 1.00034 * (_ctx_1024t + 0.3 * jax.random.normal(jax.random.fold_in(_rk, 611), (8, 1500, 128), jnp.float32))
        _g = jax.random.normal(jax.random.fold_in(_rk, 9001), (2, 2), jnp.float32)
        _g = jnp.sign(_g) * jnp.maximum(jnp.abs(_g), 1.0) + (_g == 0) * 1.0
        g_xattn = _g[0]
        g_ffn = _g[1]
        return (x, ctx_1024, g_xattn, g_ffn)
    x, ctx_1024, g_xattn, g_ffn = _rec_inputs()

    def _L0_xattn_setup():
        import jax, jax.numpy as jnp
        import numpy as np
        from jax import lax
        BIG = jnp.float32(1e+30)

        def _pairwise_euclidean(a, b):
            aa = jnp.sum(a * a, axis=-1)[:, None]
            bb = jnp.sum(b * b, axis=-1)[None, :]
            ab = a @ b.T
            return jnp.sqrt(jnp.maximum(aa + bb - 2.0 * ab, 0.0))

        def _dtw_cost(D):
            row0 = jnp.cumsum(D[0])

            def row_step(prev_row, d_row):
                first = d_row[0] + prev_row[0]

                def col_step(left, inp):
                    d_ij, up, diag = inp
                    r = d_ij + jnp.minimum(jnp.minimum(up, left), diag)
                    return (r, r)
                _, rest = lax.scan(col_step, first, (d_row[1:], prev_row[1:], prev_row[:-1]))
                row = jnp.concatenate([first[None], rest])
                return (row, row)
            _, rows = lax.scan(row_step, row0, D[1:])
            return jnp.concatenate([row0[None], rows], axis=0)

        def _backtrack(R, T1, T2):
            L = T1 + T2 - 1

            def step(carry, _):
                i, j, done = carry
                valid = jnp.logical_not(done)
                cd = jnp.where((i > 0) & (j > 0), R[jnp.maximum(i - 1, 0), jnp.maximum(j - 1, 0)], BIG)
                cu = jnp.where(i > 0, R[jnp.maximum(i - 1, 0), j], BIG)
                cl = jnp.where(j > 0, R[i, jnp.maximum(j - 1, 0)], BIG)
                choice = jnp.argmin(jnp.stack([cd, cu, cl]))
                ni = jnp.where(choice <= 1, i - 1, i)
                nj = jnp.where((choice == 0) | (choice == 2), j - 1, j)
                at_origin = (i == 0) & (j == 0)
                ni = jnp.where(at_origin, 0, ni)
                nj = jnp.where(at_origin, 0, nj)
                return ((ni, nj, done | at_origin), (i, j, valid))
            init = (jnp.int32(T1 - 1), jnp.int32(T2 - 1), jnp.bool_(False))
            _, (i_idx, j_idx, valid) = lax.scan(step, init, None, length=L)
            return (i_idx, j_idx, valid)

        def _align_one(small, large):
            T_small, d = small.shape
            T_large = large.shape[0]
            D = _pairwise_euclidean(small, large)
            R = _dtw_cost(D)
            i_idx, j_idx, valid = _backtrack(R, T_small, T_large)
            contrib = small[i_idx] * valid[:, None].astype(small.dtype)
            expanded = jnp.zeros((T_large, d), dtype=small.dtype).at[j_idx].add(contrib)
            return expanded
        key = jax.random.key(seed)
        k1, k2 = jax.random.split(key)
        teacher = jax.random.normal(k1, (16, 50, 128), dtype=jnp.float32)
        student = jax.random.normal(k2, (16, 75, 128), dtype=jnp.float32)
        return {'teacher_features': teacher, 'student_features': student}
    _L0_xattn_all = _L0_xattn_setup()
    _L0_xattn_in = {k: v for k, v in _L0_xattn_all.items() if k in ()}
    del _L0_xattn_all

    def _L0_ffn_setup():
        import jax, jax.numpy as jnp
        import numpy as np
        EPS = 1e-12

        def rms_norm(t, gamma):
            n = jnp.maximum(jnp.linalg.norm(t, axis=-1, keepdims=True), EPS)
            scale = jnp.sqrt(jnp.asarray(t.shape[-1], t.dtype))
            return t / n * scale * gamma
        key = jax.random.key(seed)
        ks = jax.random.split(key, 4)
        b, s, d = (4, 512, 128)
        e, t = (8, 64)
        hidden = 4 * d
        return {'x': jax.random.normal(ks[0], (b, s, d), dtype=jnp.float32), 'gamma_x': jnp.ones((d,), dtype=jnp.float32), 'gamma_slot': jnp.ones((d,), dtype=jnp.float32), 'slot_embeds': jax.random.normal(ks[1], (e, t, d), dtype=jnp.float32), 'w1': jax.random.normal(ks[2], (d, hidden), dtype=jnp.float32) * (1.0 / np.sqrt(d)), 'w2': jax.random.normal(ks[3], (hidden, d), dtype=jnp.float32) * (1.0 / np.sqrt(hidden))}
    _L0_ffn_all = _L0_ffn_setup()
    _L0_ffn_in = {k: v for k, v in _L0_ffn_all.items() if k in ('gamma_x', 'gamma_slot', 'slot_embeds', 'w1', 'w2')}
    del _L0_ffn_all

    def _L1_xattn_setup():
        import jax, jax.numpy as jnp
        import numpy as np
        D1, D2, D3 = (128, 128, 128)
        key = jax.random.key(seed)
        k1, k2, kw, kb = jax.random.split(key, 4)
        x1 = jax.random.normal(k1, (8, 256, D1), dtype=jnp.float32)
        x2 = jax.random.normal(k2, (8, 256, D2), dtype=jnp.float32)
        bound = 1.0 / np.sqrt(D1 + D2)
        W = jax.random.uniform(kw, (D3, D1 + D2), minval=-bound, maxval=bound, dtype=jnp.float32)
        b = jax.random.uniform(kb, (D3,), minval=-bound, maxval=bound, dtype=jnp.float32)
        return {'x1': x1, 'x2': x2, 'W': W, 'b': b}
    _L1_xattn_all = _L1_xattn_setup()
    _L1_xattn_in = {k: v for k, v in _L1_xattn_all.items() if k in ('W', 'b')}
    del _L1_xattn_all

    def _L1_ffn_setup():
        import jax, jax.numpy as jnp
        import numpy as np
        TOP_K = 2
        key = jax.random.key(seed)
        ks = jax.random.split(key, 8)
        B, S, D, E = (4, 256, 128, 8)
        H = 4 * D
        x = jax.random.normal(ks[0], (B, S, D), dtype=jnp.float32)
        W1 = jax.random.normal(ks[1], (E, D, H), dtype=jnp.float32) * np.sqrt(2.0 / (D + H))
        b1 = jax.random.normal(ks[2], (E, H), dtype=jnp.float32) * 1e-06
        W2 = jax.random.normal(ks[3], (E, H, D), dtype=jnp.float32) * np.sqrt(2.0 / (H + D))
        b2 = jax.random.normal(ks[4], (E, D), dtype=jnp.float32) * 1e-06
        gate_w = jax.random.normal(ks[5], (D, E), dtype=jnp.float32) * np.sqrt(1.0 / D)
        gate_b = jnp.zeros((E,), dtype=jnp.float32)
        temperature = jnp.asarray(1.0, dtype=jnp.float32)
        return {'x': x, 'W1': W1, 'b1': b1, 'W2': W2, 'b2': b2, 'gate_w': gate_w, 'gate_b': gate_b, 'temperature': temperature}
    _L1_ffn_all = _L1_ffn_setup()
    _L1_ffn_in = {k: v for k, v in _L1_ffn_all.items() if k in ('W1', 'b1', 'W2', 'b2', 'gate_w', 'gate_b', 'temperature')}
    del _L1_ffn_all
    return {'x': x, 'ctx_1024': ctx_1024, 'g_xattn': g_xattn, 'g_ffn': g_ffn, 'L0_ffn_gamma_x': _L0_ffn_in['gamma_x'], 'L0_ffn_gamma_slot': _L0_ffn_in['gamma_slot'], 'L0_ffn_slot_embeds': _L0_ffn_in['slot_embeds'], 'L0_ffn_w1': _L0_ffn_in['w1'], 'L0_ffn_w2': _L0_ffn_in['w2'], 'L1_xattn_W': _L1_xattn_in['W'], 'L1_xattn_b': _L1_xattn_in['b'], 'L1_ffn_W1': _L1_ffn_in['W1'], 'L1_ffn_b1': _L1_ffn_in['b1'], 'L1_ffn_W2': _L1_ffn_in['W2'], 'L1_ffn_b2': _L1_ffn_in['b2'], 'L1_ffn_gate_w': _L1_ffn_in['gate_w'], 'L1_ffn_gate_b': _L1_ffn_in['gate_b'], 'L1_ffn_temperature': _L1_ffn_in['temperature']}

def reference(x, ctx_1024, g_xattn, g_ffn, L0_ffn_gamma_x, L0_ffn_gamma_slot, L0_ffn_slot_embeds, L0_ffn_w1, L0_ffn_w2, L1_xattn_W, L1_xattn_b, L1_ffn_W1, L1_ffn_b1, L1_ffn_W2, L1_ffn_b2, L1_ffn_gate_w, L1_ffn_gate_b, L1_ffn_temperature):
    import jax
    import jax.numpy as jnp

    def _L0_xattn_ref(teacher_features, student_features):
        import jax, jax.numpy as jnp
        import numpy as np
        from jax import lax
        BIG = jnp.float32(1e+30)

        def _pairwise_euclidean(a, b):
            aa = jnp.sum(a * a, axis=-1)[:, None]
            bb = jnp.sum(b * b, axis=-1)[None, :]
            ab = a @ b.T
            return jnp.sqrt(jnp.maximum(aa + bb - 2.0 * ab, 0.0))

        def _dtw_cost(D):
            row0 = jnp.cumsum(D[0])

            def row_step(prev_row, d_row):
                first = d_row[0] + prev_row[0]

                def col_step(left, inp):
                    d_ij, up, diag = inp
                    r = d_ij + jnp.minimum(jnp.minimum(up, left), diag)
                    return (r, r)
                _, rest = lax.scan(col_step, first, (d_row[1:], prev_row[1:], prev_row[:-1]))
                row = jnp.concatenate([first[None], rest])
                return (row, row)
            _, rows = lax.scan(row_step, row0, D[1:])
            return jnp.concatenate([row0[None], rows], axis=0)

        def _backtrack(R, T1, T2):
            L = T1 + T2 - 1

            def step(carry, _):
                i, j, done = carry
                valid = jnp.logical_not(done)
                cd = jnp.where((i > 0) & (j > 0), R[jnp.maximum(i - 1, 0), jnp.maximum(j - 1, 0)], BIG)
                cu = jnp.where(i > 0, R[jnp.maximum(i - 1, 0), j], BIG)
                cl = jnp.where(j > 0, R[i, jnp.maximum(j - 1, 0)], BIG)
                choice = jnp.argmin(jnp.stack([cd, cu, cl]))
                ni = jnp.where(choice <= 1, i - 1, i)
                nj = jnp.where((choice == 0) | (choice == 2), j - 1, j)
                at_origin = (i == 0) & (j == 0)
                ni = jnp.where(at_origin, 0, ni)
                nj = jnp.where(at_origin, 0, nj)
                return ((ni, nj, done | at_origin), (i, j, valid))
            init = (jnp.int32(T1 - 1), jnp.int32(T2 - 1), jnp.bool_(False))
            _, (i_idx, j_idx, valid) = lax.scan(step, init, None, length=L)
            return (i_idx, j_idx, valid)

        def _align_one(small, large):
            T_small, d = small.shape
            T_large = large.shape[0]
            D = _pairwise_euclidean(small, large)
            R = _dtw_cost(D)
            i_idx, j_idx, valid = _backtrack(R, T_small, T_large)
            contrib = small[i_idx] * valid[:, None].astype(small.dtype)
            expanded = jnp.zeros((T_large, d), dtype=small.dtype).at[j_idx].add(contrib)
            return expanded
        return jax.vmap(_align_one)(teacher_features, student_features)

    def _L0_ffn_ref(x, gamma_x, gamma_slot, slot_embeds, w1, w2):
        import jax, jax.numpy as jnp
        import numpy as np
        EPS = 1e-12

        def rms_norm(t, gamma):
            n = jnp.maximum(jnp.linalg.norm(t, axis=-1, keepdims=True), EPS)
            scale = jnp.sqrt(jnp.asarray(t.shape[-1], t.dtype))
            return t / n * scale * gamma
        b, s, d = x.shape
        e, t, _ = slot_embeds.shape
        xn = rms_norm(x, gamma_x)
        se = rms_norm(slot_embeds, gamma_slot)
        logits = jnp.einsum('bsd,etd->bset', xn, se)
        dispatch = jax.nn.softmax(logits, axis=1)
        slots = jnp.einsum('bsd,bset->betd', xn, dispatch)
        h = jax.nn.gelu(slots @ w1, approximate=False)
        processed = h @ w2
        combine = jax.nn.softmax(logits.reshape(b, s, e * t), axis=-1)
        out = jnp.einsum('bnd,bsn->bsd', processed.reshape(b, e * t, d), combine)
        return out

    def _L1_xattn_ref(x1, x2, W, b):
        import jax, jax.numpy as jnp
        import numpy as np
        D1, D2, D3 = (128, 128, 128)
        d1 = x1.shape[-1]
        W1 = W[:, :d1]
        W2 = W[:, d1:]
        part1 = jnp.einsum('bld,ed->ble', x1, W1)
        part2 = jnp.einsum('bld,ed->be', x2, W2) / x2.shape[1]
        return part1 + part2[:, None, :] + b

    def _L1_ffn_ref(x, W1, b1, W2, b2, gate_w, gate_b, temperature):
        import jax, jax.numpy as jnp
        import numpy as np
        TOP_K = 2
        gates = (jnp.einsum('bsd,de->bse', x, gate_w) + gate_b) / temperature
        weights, indices = jax.lax.top_k(gates, TOP_K)
        weights = jax.nn.softmax(weights, axis=-1)
        h = jnp.einsum('bsd,edf->bsef', x, W1) + b1
        h = jax.nn.gelu(h, approximate=False)
        all_out = jnp.einsum('bsef,efd->bsed', h, W2) + b2
        expert_out = jnp.take_along_axis(all_out, indices[..., None], axis=2)
        out = jnp.sum(expert_out * weights[..., None], axis=2)
        return out
    x = x + jnp.tanh(g_xattn[0]) * _L0_xattn_ref(ctx_1024, _layernorm(x, axis=-1))
    x = x + jnp.tanh(g_ffn[0]) * _L0_ffn_ref(_layernorm(x, axis=-1), L0_ffn_gamma_x, L0_ffn_gamma_slot, L0_ffn_slot_embeds, L0_ffn_w1, L0_ffn_w2)
    x = x + jnp.tanh(g_xattn[1]) * _L1_xattn_ref(_layernorm(x, axis=-1), ctx_1024, L1_xattn_W, L1_xattn_b)
    x = x + jnp.tanh(g_ffn[1]) * _L1_ffn_ref(_layernorm(x, axis=-1), L1_ffn_W1, L1_ffn_b1, L1_ffn_W2, L1_ffn_b2, L1_ffn_gate_w, L1_ffn_gate_b, L1_ffn_temperature)
    return x

_drawn_inputs = setup_inputs


def setup_inputs(seed=0):
    import zlib

    import numpy as np

    out = dict(_drawn_inputs(seed))
    spreads = {'g_ffn': (-1.0, 0.6),
     'L0_ffn_gamma_x': (1.0, 0.6),
     'L0_ffn_gamma_slot': (1.0, 0.6),
     'L1_ffn_gate_b': (0.0, 0.8)}
    factors = {'L0_ffn_slot_embeds': 8.0,
     'L0_ffn_w1': 7.192,
     'L0_ffn_w2': 6.516,
     'L1_xattn_W': 7.824,
     'L1_xattn_b': 42.455,
     'L1_ffn_W1': 8.0,
     'L1_ffn_b1': 64.0,
     'L1_ffn_W2': 8.0,
     'L1_ffn_b2': 64.0,
     'L1_ffn_gate_w': 8.0}
    for name, (base, spread) in spreads.items():
        noise = np.random.default_rng([zlib.crc32(name.encode()), seed]).standard_normal(out[name].shape)
        drawn = base * np.exp(spread * noise) if base else spread * noise
        out[name] = jnp.asarray(drawn.astype(out[name].dtype))
    for name, factor in factors.items():
        out[name] = (out[name] * factor).astype(out[name].dtype)
    return out
```

```python
from contextlib import ExitStack

import concourse.bass as bass
from concourse import mybir

F32 = mybir.dt.float32
BF16 = mybir.dt.bfloat16
I32 = mybir.dt.int32
ALU = mybir.AluOpType
ACT = mybir.ActivationFunctionType
AX = mybir.AxisListType

P = 128
LN_EPS = 1e-5
RMS_EPS = 1e-12
INF = 1e30
PAD_D2 = 1e35


def gated_stack(nc, x, ctx_in, g_xattn, g_ffn, gamma_x, gamma_slot, slot_embeds, w1, w2, Wc, bc,
                eW1, eb1, eW2, eb2, gate_w, gate_b, temperature, out):
    B, S, D = x.shape
    L = ctx_in.shape[1]
    LPB = P // B
    C = LPB - 1
    N = L // C
    R = N + 1
    STEPS = S + C - 1
    TT = B // 2
    SP = P // 2
    NS, NT, _ = slot_embeds.shape
    SLOTS = NS * NT
    KS = SLOTS // P
    HID = w1.shape[1]
    Q = HID // P
    E = eW1.shape[0]
    assert D == P and C * N == L and B * LPB == P and S <= SP
    LAST_KEY = 4 * L
    TG = 5
    GPB = C // TG
    NG = B * GPB
    HALVES = ((0, 8), (8, C))
    DG = 5
    ND = STEPS // DG

    with ExitStack() as stack:
        def sb(name, shape, dt=F32):
            return stack.enter_context(nc.sbuf_tensor(name, shape, dt))

        def sem(name):
            return stack.enter_context(nc.semaphore(name))

        ctx_n = sb("ctx_n", [P, B * C, D])
        region_x = sb("region_x", [P, B * L])
        ctx_t = region_x[:, :].rearrange("p (g n) -> p g n", n=N)
        key_t = region_x[:, 0:STEPS * N].rearrange("p (s n) -> p s n", n=N)
        ew1_s = region_x[:, 7040:7040 + E * HID].rearrange("p (e f) -> p e f", e=E)
        disp_e = region_x[:, 0:KS * B * SP].rearrange("p (k b s) -> p k b s", k=KS, b=B)
        comb_e = region_x[:, 2048:2048 + TT * SLOTS].rearrange("p (t n) -> p t n", t=TT)
        xw_s = region_x[:, 4096:4096 + TT * HID].rearrange("p (t f) -> p t f", t=TT)
        ht_s = region_x[:, 0:2 * Q * B * SP].rearrange("p (r q n) -> p r q n", r=2, q=Q)
        region_d = sb("region_d", [P, STEPS * P])
        prod = region_d[:, :].rearrange("p (s l) -> p s l", l=P)
        left_f = region_d[:, 0:STEPS * N // 2].bitcast(BF16).rearrange("p (s n) -> p s n", n=N)
        diag_f = region_d[:, 3520:3520 + STEPS * N // 2].bitcast(BF16).rearrange("p (s n) -> p s n", n=N)
        mask = region_d[:, 0:C * B * SP].rearrange("p (c b s) -> p c b s", c=C, b=B)
        under = region_d[:, 7680:7680 + 2 * B * S].rearrange("p (r b s) -> p r b s", r=2, b=B)
        acc = region_d[:, 0:TT * D].rearrange("p (t d) -> p t d", t=TT)
        wt_t = region_d[0:E, 512:512 + TT * P]
        disp_t = region_d[:, 0:TT * SLOTS].rearrange("p (t n) -> p t n", t=TT)
        comb_t = region_d[:, 2048:2048 + KS * B * SP].rearrange("p (k n) -> p k n", k=KS)
        NHR = 4
        h_s = region_d[:, 4096:4096 + NHR * HID].rearrange("p (r f) -> p r f", r=NHR)
        y_t = region_d[:, 6144:6144 + Q * B * SP].rearrange("p (q n) -> p q n", q=Q)
        region_w = sb("region_w", [P, (STEPS + 1) * R])
        cost = region_w[:, :].rearrange("p (s r) -> p s r", r=R)
        ew2_s = region_w[:, 0:E * HID].rearrange("p (e q d) -> p e q d", e=E, q=Q)

        x_s = sb("x_s", [P, TT, D])
        xn_s = sb("xn_s", [P, TT, D])
        xt_s = sb("xt_s", [P, B * SP])
        xsq_s = sb("xsq_s", [P, B * SP])
        bb_s = sb("bb_s", [P, B, SP])
        stats = sb("stats", [P, TT, 6])
        mv = sb("mv", [P, TT, 2])
        vv = sb("vv", [P, 2, TT])
        vr = sb("vr", [P, 2, TT])
        den = sb("den", [P, TT])
        fac = sb("fac", [P, TT])
        half = sb("half", [P, 2 * TT])
        mhalf = sb("mhalf", [P, TT])
        ident = sb("ident", [P, P])
        ones = sb("ones", [P, P])
        aa_n = sb("aa_n", [P, P])
        aa_l = sb("aa_l", [P, N])
        junk_v = sb("junk_v", [P, 2, D])
        junk_a = sb("junk_a", [P, 2, D])
        lane_i = sb("lane_i", [P, 1], I32)
        lane_m = sb("lane_m", [P, 1], I32)
        lane_f = sb("lane_f", [P, 1])
        lane4 = sb("lane4", [P, 1])
        lane0 = sb("lane0", [P, 1])
        key_row = sb("key_row", [P, N])
        key4 = sb("key4", [P, N])
        m_s = sb("m_s", [P, 2, N])
        hit = sb("hit", [P, 2, R])
        keys = sb("keys", [P, STEPS + 1])
        lane_sel = sb("lane_sel", [P, B, N])
        keys_b = sb("keys_b", [P, B, S + 1])
        row4 = sb("row4", [P, C])
        row4b = sb("row4b", [P, C])
        csum_g = sb("csum_g", [P, B, GPB])
        csum = sb("csum", [P, B])
        csum_b = sb("csum_b", [P, B, SP])
        gx_b = sb("gx_b", [P, 2])
        gf_b = sb("gf_b", [P, 2])
        tgx = sb("tgx", [P, 2])
        tgf = sb("tgf", [P, 2])
        tgr = sb("tgr", [P, TT])
        gam_x = sb("gam_x", [P, 1])
        gam_s = sb("gam_s", [P, 1])
        se_n = sb("se_n", [P, KS, D])
        se_sq = sb("se_sq", [P, KS])
        se_r = sb("se_r", [P, KS])
        se_t = sb("se_t", [P, SLOTS])
        w1_s = sb("w1_s", [P, HID])
        w2_s = sb("w2_s", [P, Q, D])
        wc_n = sb("wc_n", [P, 2, D])
        wc_t = sb("wc_t", [P, 2, D])
        bc_s = sb("bc_s", [1, D])
        b1_n = sb("b1_n", [E * Q, P])
        b1_t = sb("b1_t", [P, E * Q])
        b2_s = sb("b2_s", [E, D])
        gw_s = sb("gw_s", [P, E])
        gb_s = sb("gb_s", [1, E])
        temp_s = sb("temp_s", [P, 1])
        rtemp = sb("rtemp", [P, 1])
        d_max = sb("d_max", [P, KS, B])
        d_sum = sb("d_sum", [P, KS, B])
        d_inv = sb("d_inv", [P, KS, B])
        c_nmax = sb("c_nmax", [P, TT])
        c_sum = sb("c_sum", [P, TT])
        c_inv = sb("c_inv", [P, TT])
        gates = sb("gates", [P, TT, E])
        top = sb("top", [P, TT, 8])
        top_i = sb("top_i", [P, TT, 8], mybir.dt.uint32)
        top_f = sb("top_f", [P, TT, 2])
        e_iota = sb("e_iota", [P, E])
        gdiff = sb("gdiff", [P, TT])
        gexp = sb("gexp", [P, TT])
        gden = sb("gden", [P, TT])
        wgt = sb("wgt", [P, 2, TT])
        wt1 = sb("wt1", [P, TT, E])
        wt2 = sb("wt2", [P, TT, E])
        wt = sb("wt", [P, TT, E])

        ps = stack.enter_context(nc.psum_tensor("ps", [P, 8, 512], F32))

        x_in = sem("x_in")
        small_in = sem("small_in")
        ctx_part = [sem(f"ctx_in{b}") for b in range(B)]
        ew1_in = sem("ew1_in")
        ew2_in = sem("ew2_in")
        out_done = sem("out_done")
        zeroed = sem("zeroed")
        consts = sem("consts")
        pads = sem("pads")
        pool_pow = sem("pool_pow")
        var_up = sem("var_up")
        dve_c = sem("dve_c")
        xn_up = sem("xn_up")
        xt_ps = sem("xt_ps")
        xt_up = sem("xt_up")
        bb_ps = sem("bb_ps")
        bb_up = sem("bb_up")
        small_ps = sem("small_ps")
        small_up = sem("small_up")
        se_up = sem("se_up")
        ctx_ps = sem("ctx_ps")
        ctx_up = sem("ctx_up")
        prod_ps = sem("prod_ps")
        prod_up = sem("prod_up")
        aa_up = sem("aa_up")
        aa_ps = sem("aa_ps")
        aal_up = sem("aal_up")
        dist_ps = sem("dist_ps")
        dist2_up = sem("dist2_up")
        dist_up = sem("dist_up")
        wave_m = sem("wave_m")
        wave_r = sem("wave_r")
        flags_up = sem("flags_up")
        gap_up = sem("gap_up")
        sign_up = sem("sign_up")
        key_up = sem("key_up")
        pick_up = sem("pick_up")
        hit_up = sem("hit_up")
        keys_up = sem("keys_up")
        kb_ps = sem("kb_ps")
        mask_up = sem("mask_up")
        exp_ps = sem("exp_ps")
        csum_up = sem("csum_up")
        tg_up = sem("tg_up")
        xw_ps = sem("xw_ps")
        xw_up = sem("xw_up")
        ld_ps = sem("ld_ps")
        ld_sub = sem("ld_sub")
        ld_exp = sem("ld_exp")
        lc_ps = sem("lc_ps")
        lc_max = sem("lc_max")
        lc_exp = sem("lc_exp")
        d_inv_up = sem("d_inv_up")
        disp_ps = sem("disp_ps")
        disp_up = sem("disp_up")
        comb_ps = sem("comb_ps")
        comb_up = sem("comb_up")
        h_ps = sem("h_ps")
        h_up = sem("h_up")
        y_up = sem("y_up")
        hy_used = sem("hy_used")
        f0_ps = sem("f0_ps")
        xa_ps = sem("xa_ps")
        g_ps = sem("g_ps")
        gd_up = sem("gd_up")
        ge_up = sem("ge_up")
        wt_up = sem("wt_up")
        wtt_ps = sem("wtt_ps")
        wtt_up = sem("wtt_up")
        b2_ps = sem("b2_ps")
        eh_ps = sem("eh_ps")
        eh_up = sem("eh_up")
        eo_ps = sem("eo_ps")
        eo_up = sem("eo_up")
        fin_up = sem("fin_up")
        pads2 = sem("pads2")
        aa_act = sem("aa_act")
        flags_d = sem("flags_d")
        wave_b = sem("wave_b")
        merge_up = sem("merge_up")
        hit_b = sem("hit_b")
        under_up = sem("under_up")
        acc_up = sem("acc_up")
        se_sum = sem("se_sum")
        se_root = sem("se_root")

        def bank(i):
            return ps[:, i, :]

        def tokens(ap):
            return ap.rearrange("p (b s) -> p b s", b=B)[:, :, 0:S]

        def lane(b, c):
            return LPB * b + 1 + c

        def diagonal(b, c0, c1):
            base = prod[0:N, c0, lane(b, c0):lane(b, c0) + 1]
            return bass.AP(tensor=base.tensor, offset=base.offset,
                           ap=[list(base.ap[0]), [P + 1, c1 - c0], [P, S]])

        SMALL_ALL = 16 * 14
        CONSTS = 7
        ACT_SQ = 5

        block = stack.enter_context(nc.Block())

        @block.sync
        def _(sp):
            sp.wait_ge(zeroed, 1)
            for h in range(2):
                sp.dma_start(x_s[SP * h:SP * h + S, :, :],
                             x[h::2, :, :].rearrange("t s d -> s t d")).then_inc(x_in, 16)
            for b in range(B):
                src = ctx_in[b, :, :].rearrange("(c p) d -> p c d", p=N)
                for p0, p1 in ((0, 96), (96, N)):
                    sp.dma_start(ctx_n[p0:p1, C * b:C * b + C, :], src[p0:p1, :, :]).then_inc(ctx_part[b], 16)
            sp.wait_ge(prod_ps, 2 * B)
            sp.dma_start(ew1_s, eW1.rearrange("e d f -> d e f")).then_inc(ew1_in, 16)
            sp.wait_ge(flags_up, STEPS)
            sp.wait_ge(gap_up, ND)
            sp.dma_start(ew2_s, eW2.rearrange("e (q p) d -> p e q d", p=P)).then_inc(ew2_in, 16)
            for t in range(TT):
                sp.wait_ge(fin_up, t + 1)
                for h in range(2):
                    sp.dma_start(out[2 * t + h, :, :], x_s[SP * h:SP * h + S, t, :]).then_inc(out_done, 16)
            sp.wait_ge(out_done, 16 * 2 * TT)

        @block.gpsimd
        def _(pool):
            g = nc.gpsimd
            g.memset(ident[:, :], 0.0).then_inc(consts, 1)
            g.memset(ones[:, :], 1.0).then_inc(consts, 1)
            pool.wait_ge(consts, 2)
            g.affine_select(out=ident[:, :], in_=ident[:, :], compare_op=ALU.not_equal, fill=1.0, base=0,
                            pattern=[[-1, P]], channel_multiplier=1).then_inc(consts, 1)
            g.memset(half[:, :], 0.5).then_inc(consts, 1)
            g.memset(mhalf[:, :], -0.5).then_inc(consts, 1)
            g.iota(lane_i[:, :], pattern=[[0, 1]], base=0, channel_multiplier=1).then_inc(consts, 1)
            g.iota(key_row[:, :], pattern=[[4, N]], base=-4 * N, channel_multiplier=0,
                   allow_small_or_imprecise_dtypes=True).then_inc(consts, 1)
            pool.wait_ge(var_up, 1)
            g.tensor_tensor(vr[:, 0, :], vv[:, 1, :], mhalf[:, :], ALU.pow).then_inc(pool_pow, 1)
            g.memset(prod[:, 0:C - 1, :], PAD_D2).then_inc(pads, 1)
            g.memset(prod[:, S:STEPS, :], PAD_D2).then_inc(pads, 1)
            g.memset(prod[:, C - 1:S, 0:P:LPB], PAD_D2).then_inc(pads, 1)
            g.memset(aa_n[:, :], 0.0).then_inc(pads, 1)
            g.memset(lane_sel[:, :, :], 0.0).then_inc(pads, 1)
            pool.wait_ge(pads, 5)
            g.affine_select(out=lane_sel[:, :, :], in_=lane_sel[:, :, :], compare_op=ALU.not_equal, fill=1.0,
                            base=-1, pattern=[[-LPB, B], [0, N]], channel_multiplier=1).then_inc(pads2, 1)
            g.iota(row4[:, :], pattern=[[4 * N, C]], base=0, channel_multiplier=4,
                   allow_small_or_imprecise_dtypes=True).then_inc(pads2, 1)
            g.iota(row4b[:, :], pattern=[[4 * N, C]], base=2, channel_multiplier=4,
                   allow_small_or_imprecise_dtypes=True).then_inc(pads2, 1)
            g.iota(e_iota[:, :], pattern=[[1, E]], base=0, channel_multiplier=0,
                   allow_small_or_imprecise_dtypes=True).then_inc(pads2, 1)
            pool.wait_ge(prod_ps, 2 * B)

            def finish_keys(n):
                pool.wait_ge(sign_up, n + 1)
                rows = key_t[:, DG * n:DG * n + DG, :]
                g.tensor_tensor(rows, rows, key4[:, None, :].to_broadcast([P, DG, N]), ALU.add).then_inc(key_up, 1)

            pool.wait_ge(dve_c, 5)
            for n in range(ND):
                pool.wait_ge(wave_r, DG * n + DG - 1)
                rows = cost[:, DG * n:DG * n + DG, :]
                g.tensor_tensor(key_t[:, DG * n:DG * n + DG, :], rows[:, :, 0:N], rows[:, :, 1:R],
                                ALU.subtract).then_inc(gap_up, 1)
                if n >= 1:
                    finish_keys(n - 1)
            finish_keys(ND - 1)
            for n in range(1, 4):
                pool.wait_ge(var_up, n + 1)
                if n == 1:
                    g.tensor_tensor(vr[:, :, :].rearrange("p a t -> p (a t)"),
                                    vv[:, :, :].rearrange("p a t -> p (a t)"), half[:, :], ALU.pow).then_inc(pool_pow, 1)
                else:
                    g.tensor_tensor(vr[:, 0, :], vv[:, 1, :], mhalf[:, :], ALU.pow).then_inc(pool_pow, 1)
                if n == 1:
                    pool.wait_ge(exp_ps, 1)
                    g.memset(disp_e[:, :, :, S:SP], 0.0).then_inc(pads2, 1)
                    g.memset(y_t.rearrange("p q (b s) -> p q b s", b=B)[:, :, :, S:SP], 0.0).then_inc(pads2, 1)
                if n == 2:
                    pool.wait_ge(hy_used, B * KS)
                    g.memset(ht_s.rearrange("p r q (b s) -> p (r q b) s", b=B)[:, :, S:SP], 0.0).then_inc(pads2, 1)

        @block.scalar
        def _(act):
            a = nc.scalar
            for dst, src in (
                (gx_b[:, :], g_xattn.unsqueeze(0).to_broadcast([P, 2])),
                (gf_b[:, :], g_ffn.unsqueeze(0).to_broadcast([P, 2])),
                (se_n[:, :, :], slot_embeds.rearrange("e t d -> (e t) d").rearrange("(k p) d -> p k d", p=P)),
                (wc_n[:, :, :], Wc.rearrange("e (h d) -> e h d", h=2)),
                (b1_n[:, :], eb1.rearrange("e (q p) -> (e q) p", p=P)),
                (gam_x[:, :], gamma_x.unsqueeze(1)),
                (gam_s[:, :], gamma_slot.unsqueeze(1)),
                (bc_s[:, :], bc.unsqueeze(0)),
                (w1_s[:, :], w1),
                (w2_s[:, :, :], w2.rearrange("(q p) d -> p q d", p=P)),
                (b2_s[:, :], eb2),
                (gw_s[:, :], gate_w),
                (gb_s[:, :], gate_b.unsqueeze(0)),
                (temp_s[:, :], temperature.unsqueeze(0).to_broadcast([P, 1])),
            ):
                act.dma_start(dst, src).then_inc(small_in, 16)
            act.wait_ge(small_in, SMALL_ALL)
            a.activation(tgx[:, :], gx_b[:, :], ACT.Tanh).then_inc(tg_up, 1)
            a.activation(tgf[:, :], gf_b[:, :], ACT.Tanh).then_inc(tg_up, 1)
            act.wait_ge(xt_ps, 1)
            a.activation(xt_s[:, :], bank(6), ACT.Copy, scale=-2.0).then_inc(xt_up, 1)
            a.activation(xsq_s[:, :], bank(6), ACT.Square).then_inc(xt_up, 1)
            act.wait_ge(bb_ps, 1)
            a.activation(bb_s[0:N, :, :].rearrange("p b s -> p (b s)"), bank(6)[0:N, :], ACT.Copy).then_inc(bb_up, 1)

            nsq = [0]
            for k in range(NG):
                act.wait_ge(ctx_ps, k + 1)
                a.activation(region_x[:, k * TG * N:(k + 1) * TG * N], bank(k % 3)[:, 0:TG * N], ACT.Copy,
                             accum_out=csum_g[:, k // GPB, k % GPB:k % GPB + 1]).then_inc(ctx_up, 1)
                b = k // GPB
                if k % GPB == 2:
                    if b == 0:
                        act.wait_ge(pads, 5)
                    for c in range(ACT_SQ):
                        if nsq[0] >= 2:
                            act.wait_ge(aa_act, nsq[0] - 1)
                        a.activation(junk_a[0:N, nsq[0] % 2, :], ctx_n[0:N, C * b + c, :], ACT.Square,
                                     accum_out=aa_n[0:N, lane(b, c):lane(b, c) + 1]).then_inc(aa_act, 1)
                        nsq[0] += 1
            act.wait_ge(aa_ps, 1)
            a.activation(aa_l[:, :], bank(6)[:, 0:N], ACT.Copy).then_inc(aal_up, 1)
            act.wait_ge(small_ps, 1)
            a.activation(wc_t[:, :, :].rearrange("p h d -> p (h d)"), bank(7)[:, 0:2 * D], ACT.Copy).then_inc(small_up, 1)
            a.activation(b1_t[:, :], bank(7)[:, 2 * D:2 * D + E * Q], ACT.Copy).then_inc(small_up, 1)
            act.wait_ge(se_sum, 1)
            a.activation(se_r[:, :], se_r[:, :], ACT.Sqrt).then_inc(se_root, 1)
            for n in range(ND):
                act.wait_ge(dist2_up, n + 1)
                rows = cost[:, 1 + DG * n:1 + DG * n + DG, 1:R]
                a.activation(rows, rows, ACT.Sqrt).then_inc(dist_up, 1)
            act.wait_ge(small_ps, 2)
            a.activation(se_t[:, :], bank(7), ACT.Copy, scale=gam_s[:, 0:1]).then_inc(small_up, 1)
            for n in range(ND):
                act.wait_ge(gap_up, n + 1)
                rows = key_t[:, DG * n:DG * n + DG, :]
                a.activation(rows, rows, ACT.Sign).then_inc(sign_up, 1)
            act.wait_ge(xt_ps, 2)
            a.activation(xt_s[:, :], bank(5), ACT.Copy, scale=gam_x[:, 0:1]).then_inc(xt_up, 1)
            for t in range(TT):
                act.wait_ge(xw_ps, t + 1)
                a.activation(xw_s[:, t, :], bank(t), ACT.Copy).then_inc(xw_up, 1)
            for k in range(KS):
                act.wait_ge(ld_sub, k + 1)
                a.activation(disp_e[:, k, :, 0:S], disp_e[:, k, :, 0:S], ACT.Exp).then_inc(ld_exp, 1)
            for t in range(TT):
                act.wait_ge(lc_max, t + 1)
                a.activation(comb_e[:, t, :], bank(t), ACT.Exp, bias=c_nmax[:, t:t + 1],
                             accum_out=c_sum[:, t:t + 1]).then_inc(lc_exp, 1)
            for t in range(TT):
                act.wait_ge(disp_ps, t + 1)
                a.activation(disp_t[:, t, :], bank(4 + t), ACT.Copy).then_inc(disp_up, 1)
            act.wait_ge(d_inv_up, 1)
            for n in range(B * KS):
                b, k = divmod(n, KS)
                act.wait_ge(h_ps, n + 1)
                if n >= NHR:
                    act.wait_ge(hy_used, n - NHR + 1)
                a.activation(h_s[:, n % NHR, :], bank(4 + n % 4), ACT.Gelu,
                             scale=d_inv[:, k, b:b + 1]).then_inc(h_up, 1)
            act.wait_ge(xt_ps, 3)
            a.activation(xt_s[:, :], bank(3), ACT.Copy).then_inc(xt_up, 1)
            act.wait_ge(xt_ps, 4)
            a.activation(xt_s[:, :], bank(5), ACT.Copy).then_inc(xt_up, 1)
            act.wait_ge(gd_up, 1)
            a.activation(gexp[:, :], gdiff[:, :], ACT.Exp).then_inc(ge_up, 1)
            for n in range(E * Q):
                e, q = divmod(n, Q)
                act.wait_ge(eh_ps, n + 1)
                if n == 0:
                    act.wait_ge(pads2, 7)
                if e >= 2 and q == 0:
                    act.wait_ge(eo_ps, e - 1)
                a.activation(tokens(ht_s[:, e % 2, q, :]), bank(n % 3)[:, 0:B * S].rearrange("p (b s) -> p b s", b=B),
                             ACT.Gelu, bias=b1_t[:, n:n + 1]).then_inc(eh_up, 1)

        @block.tensor
        def _(pe):
            T = nc.tensor
            pe.wait_ge(consts, 3)

            def transpose_tokens(n, to):
                for t in range(TT):
                    if True:
                        pe.wait_ge(xn_up, TT * (n - 1) + t + 1)
                    last = T.transpose(bank(to)[:, t * P:(t + 1) * P], xn_s[:, t, :], ident[:, :])
                last.then_inc(xt_ps, 1)

            transpose_tokens(1, 6)
            pe.wait_ge(xt_up, 2)
            T.matmul(bank(6)[0:N, :], ones[:, 0:N], xsq_s[:, :], start=True, stop=True).then_inc(bb_ps, 1)

            def transpose_ctx(b):
                pe.wait_ge(ctx_part[b], 32)
                for j in range(GPB):
                    k = GPB * b + j
                    if k >= 3:
                        pe.wait_ge(ctx_up, k - 2)
                    for i in range(TG):
                        last = T.transpose(bank(k % 3)[:, i * N:(i + 1) * N], ctx_n[0:N, C * b + TG * j + i, :],
                                           ident[0:N, 0:N])
                    last.then_inc(ctx_ps, 1)

            def products(b):
                pe.wait_ge(ctx_up, GPB * (b + 1))
                for h, (c0, c1) in enumerate(HALVES):
                    n = 2 * b + h
                    if n >= 3:
                        pe.wait_ge(prod_up, n - 2)
                    for c in range(c0, c1):
                        last = T.matmul(bank(3 + n % 3)[0:N, (c - c0) * S:(c - c0 + 1) * S], ctx_t[:, C * b + c, :],
                                        xt_s[:, SP * b:SP * b + S], start=True, stop=True)
                    last.then_inc(prod_ps, 1)

            transpose_ctx(0)
            for b in range(1, B):
                transpose_ctx(b)
                products(b - 1)
            products(B - 1)
            pe.wait_ge(aa_up, B * (C - ACT_SQ))
            pe.wait_ge(aa_act, B * ACT_SQ)
            pe.wait_ge(bb_up, 1)
            T.transpose(bank(6)[:, 0:N], aa_n[0:N, :], ident[0:N, 0:N]).then_inc(aa_ps, 1)
            pe.wait_ge(small_in, SMALL_ALL)
            for h in range(2):
                T.transpose(bank(7)[:, h * D:(h + 1) * D], wc_n[:, h, :], ident[:, :])
            T.transpose(bank(7)[:, 2 * D:2 * D + E * Q], b1_n[:, :], ident[0:E * Q, 0:E * Q]).then_inc(small_ps, 1)
            pe.wait_ge(prod_up, 2 * B)
            pe.wait_ge(pads, 5)
            for n in range(ND):
                if n >= 3:
                    pe.wait_ge(dist2_up, n - 2)
                for i in range(DG):
                    last = T.transpose(bank(n % 3)[:, i * N:(i + 1) * N], prod[0:N, DG * n + i, :], ident[0:N, 0:N])
                last.then_inc(dist_ps, 1)
            pe.wait_ge(se_up, KS)
            pe.wait_ge(small_up, 2)
            for k in range(KS):
                last = T.transpose(bank(7)[:, k * P:(k + 1) * P], se_n[:, k, :], ident[:, :])
            last.then_inc(small_ps, 1)

            pe.wait_ge(keys_up, STEPS + 1)
            pe.wait_ge(pads2, 4)
            pe.wait_ge(dist2_up, ND)
            for b in range(B):
                last = T.matmul(bank(0)[0:N, b * (S + 1):(b + 1) * (S + 1)], lane_sel[:, b, :], keys[:, 0:S + 1],
                                start=True, stop=True)
            last.then_inc(kb_ps, 1)
            pairs = ctx_n[0:N, :, :].rearrange("p (t h c) d -> p t h c d", h=2, c=C)
            for c in range(C):
                pe.wait_ge(mask_up, c + 1)
                for t in range(TT):
                    last = T.matmul(bank(1 + t)[:, 0:2 * D], mask[0:N, c, 2 * t:2 * t + 2, :].rearrange("p h s -> p (h s)"),
                                    pairs[:, t, :, c, :], start=(c == 0), stop=(c == C - 1))
            last.then_inc(exp_ps, 1)

            transpose_tokens(2, 5)
            pe.wait_ge(xt_up, 3)
            for t in range(TT):
                T.matmul(bank(t), xt_s[:, t * P:(t + 1) * P], w1_s[:, :], start=True, stop=True).then_inc(xw_ps, 1)
            pe.wait_ge(small_up, 3)
            for k in range(KS):
                T.matmul(bank(4 + k)[:, 0:B * S], se_t[:, k * P:(k + 1) * P], tokens(xt_s[:, :]),
                         start=True, stop=True).then_inc(ld_ps, 1)
            for t in range(TT):
                pe.wait_ge(xw_up, t + 1)
                T.matmul(bank(t), xt_s[:, t * P:(t + 1) * P], se_t[:, :], start=True, stop=True).then_inc(lc_ps, 1)
            pe.wait_ge(ld_exp, KS)
            pe.wait_ge(pads2, 5)
            for t in range(TT):
                for k in range(KS):
                    last = T.transpose(bank(4 + t)[:, k * P:(k + 1) * P],
                                       disp_e[:, k, 2 * t:2 * t + 2, :].rearrange("p h s -> p (h s)"), ident[:, :])
                last.then_inc(disp_ps, 1)
            pe.wait_ge(lc_exp, TT)
            for k in range(KS):
                for t in range(TT):
                    last = T.transpose(bank(k)[:, t * P:(t + 1) * P], comb_e[:, t, k * P:(k + 1) * P], ident[:, :])
                last.then_inc(comb_ps, 1)

            def hidden(n):
                b, k = divmod(n, KS)
                t, h = divmod(b, 2)
                if k == 0 and h == 0:
                    pe.wait_ge(disp_up, TT if n == 0 else t + 1)
                if n >= 4:
                    pe.wait_ge(h_up, n - 3)
                T.matmul(bank(4 + n % 4), disp_t[SP * h:SP * h + S, t, k * P:(k + 1) * P],
                         xw_s[SP * h:SP * h + S, t, :], start=True, stop=True).then_inc(h_ps, 1)

            def combined(n):
                b, k = divmod(n, KS)
                pe.wait_ge(h_up, n + 1)
                if k == 0:
                    pe.wait_ge(comb_up, KS)
                    if b >= 2:
                        pe.wait_ge(y_up, b - 1)
                for q in range(Q):
                    last = T.matmul(bank(b % 2)[:, q * S:(q + 1) * S], h_s[:, n % NHR, q * P:(q + 1) * P],
                                    comb_t[:, k, SP * b:SP * b + S], start=(k == 0 and q == 0), stop=(k == KS - 1),
                                    skip_group_check=True)
                last.then_inc(hy_used, 1)

            pe.wait_ge(xw_up, TT)
            AHEAD = 3
            for n in range(B * KS + AHEAD):
                if n < B * KS:
                    hidden(n)
                if n >= AHEAD:
                    combined(n - AHEAD)
            pe.wait_ge(y_up, B)
            pe.wait_ge(pads2, 6)
            for t in range(TT):
                for q in range(Q):
                    last = T.matmul(bank(2)[:, t * D:(t + 1) * D], y_t[:, q, t * P:(t + 1) * P], w2_s[:, q, :],
                                    start=(q == 0), stop=(q == Q - 1))
                last.then_inc(f0_ps, 1)

            transpose_tokens(3, 3)
            pe.wait_ge(small_up, 2)
            pe.wait_ge(csum_up, 1)
            for t in range(TT):
                dst = bank(4)[:, t * D:(t + 1) * D]
                T.matmul(dst, csum_b[:, 2 * t:2 * t + 2, :].rearrange("p h s -> p (h s)"), wc_t[:, 1, :],
                         start=True, stop=False)
                T.matmul(dst, ones[0:1, :], bc_s[0:1, :], start=False, stop=False)
                if t == 0:
                    pe.wait_ge(xt_up, 4)
                T.matmul(dst, xt_s[:, t * P:(t + 1) * P], wc_t[:, 0, :], start=False, stop=True).then_inc(xa_ps, 1)

            transpose_tokens(4, 5)
            pe.wait_ge(xt_up, 5)
            for t in range(TT):
                dst = bank(6)[:, t * E:(t + 1) * E]
                T.matmul(dst, xt_s[:, t * P:(t + 1) * P], gw_s[:, :], start=True, stop=False)
                last = T.matmul(dst, ones[0:1, :], gb_s[0:1, :], start=False, stop=True)
            last.then_inc(g_ps, 1)

            def expert_hidden(e):
                if e == 0:
                    pe.wait_ge(ew1_in, 16)
                for q in range(Q):
                    n = e * Q + q
                    if n >= 3:
                        pe.wait_ge(eh_up, n - 2)
                    T.matmul(bank(n % 3)[:, 0:B * S], ew1_s[:, e, q * P:(q + 1) * P], tokens(xt_s[:, :]),
                             start=True, stop=True).then_inc(eh_ps, 1)

            def expert_out(e):
                if e == 0:
                    pe.wait_ge(ew2_in, 16)
                if e >= 2:
                    pe.wait_ge(eo_up, TT * (e - 1))
                pe.wait_ge(eh_up, Q * (e + 1))
                for t in range(TT):
                    for q in range(Q):
                        last = T.matmul(bank(4 + e % 2)[:, t * D:(t + 1) * D], ht_s[:, e % 2, q, t * P:(t + 1) * P],
                                        ew2_s[:, e, q, :], start=(q == 0), stop=(q == Q - 1))
                last.then_inc(eo_ps, 1)

            def second_biases():
                pe.wait_ge(wt_up, 1)
                for t in range(TT):
                    last = T.transpose(bank(7)[0:E, t * P:(t + 1) * P], wt[:, t, :], ident[:, :])
                last.then_inc(wtt_ps, 1)
                pe.wait_ge(wtt_up, 1)
                for t in range(TT):
                    last = T.matmul(bank(3)[:, t * D:(t + 1) * D], wt_t[:, t * P:(t + 1) * P], b2_s[:, :],
                                    start=True, stop=True)
                last.then_inc(b2_ps, 1)

            expert_hidden(0)
            for e in range(E):
                if e + 1 < E:
                    expert_hidden(e + 1)
                if e == 0:
                    second_biases()
                expert_out(e)

        @block.vector
        def _(dve):
            v = nc.vector
            done = [0]

            def link(ins):
                done[0] += 1
                ins.then_inc(dve_c, 1)
                dve.wait_ge(dve_c, done[0])

            def mark(ins):
                done[0] += 1
                ins.then_inc(dve_c, 1)

            def row_stats():
                for t in range(TT):
                    mark(v.bn_stats(stats[:, t, :], x_s[:, t, :]))
                dve.wait_ge(dve_c, done[0])
                for t in range(TT):
                    mark(v.bn_aggr(mv[:, t, :], stats[:, t, :]))
                dve.wait_ge(dve_c, done[0])

            def layer_norm(n):
                row_stats()
                v.tensor_scalar(vv[:, 1, :], mv[:, :, 1], LN_EPS, None, ALU.add).then_inc(var_up, 1)
                dve.wait_ge(pool_pow, n)
                for t in range(TT):
                    v.tensor_scalar(xn_s[:, t, :], x_s[:, t, :], mv[:, t, 0:1], vr[:, 0, t:t + 1],
                                    ALU.subtract, ALU.mult).then_inc(xn_up, 1)

            v.memset(x_s[:, :, :], 0.0).then_inc(zeroed, 1)
            dve.wait_ge(consts, CONSTS)
            link(v.tensor_scalar(lane_m[:, :], lane_i[:, :], LPB - 1, None, ALU.bitwise_and))
            link(v.tensor_copy(lane_f[:, :], lane_m[:, :]))
            link(v.tensor_scalar(lane4[:, :], lane_f[:, :], 4.0 * N, None, ALU.mult))
            mark(v.memset(cost[:, 0, :], INF))
            link(v.tensor_scalar(key4[:, :], key_row[:, :], lane4[:, 0:1], None, ALU.add))
            assert done[0] == 5
            link(v.tensor_scalar(lane0[:, :], lane_f[:, :], 1.0, -INF, ALU.is_equal, ALU.mult))
            link(v.tensor_scalar(cost[:, 0, 0:1], lane0[:, :], INF, None, ALU.add))
            v.tensor_scalar(keys[:, STEPS:STEPS + 1], lane_f[:, :], 0.0, float(LAST_KEY),
                            ALU.is_gt, ALU.mult).then_inc(keys_up, 1)

            dve.wait_ge(x_in, 32)
            layer_norm(1)

            nsq = [0]

            def square_sums(b):
                if b == 0:
                    dve.wait_ge(pads, 5)
                dve.wait_ge(ctx_part[b], 32)
                for c in range(ACT_SQ, C):
                    if nsq[0] >= 2:
                        dve.wait_ge(aa_up, nsq[0] - 1)
                    v.tensor_tensor_reduce(junk_v[0:N, nsq[0] % 2, :], ctx_n[0:N, C * b + c, :],
                                           ctx_n[0:N, C * b + c, :], 1.0, 0.0, ALU.mult, ALU.add,
                                           aa_n[0:N, lane(b, c):lane(b, c) + 1]).then_inc(aa_up, 1)
                    nsq[0] += 1

            def store_products(b):
                if b == 0:
                    dve.wait_ge(bb_up, 1)
                for h, (c0, c1) in enumerate(HALVES):
                    n = 2 * b + h
                    dve.wait_ge(prod_ps, n + 1)
                    v.tensor_tensor(diagonal(b, c0, c1),
                                    bank(3 + n % 3)[0:N, 0:(c1 - c0) * S].rearrange("p (c s) -> p c s", s=S),
                                    bb_s[0:N, b:b + 1, 0:S].to_broadcast([N, c1 - c0, S]), ALU.add).then_inc(prod_up, 1)

            square_sums(0)
            for b in range(1, B):
                square_sums(b)
                store_products(b - 1)
            store_products(B - 1)

            dve.wait_ge(small_in, SMALL_ALL)
            for k in range(KS):
                if k >= 2:
                    dve.wait_ge(dve_c, done[0] - 1)
                if k == 0:
                    dve.wait_ge(aa_up, nsq[0])
                mark(v.tensor_tensor_reduce(junk_v[:, k % 2, :], se_n[:, k, :], se_n[:, k, :], 1.0, 0.0,
                                            ALU.mult, ALU.add, se_sq[:, k:k + 1]))
            dve.wait_ge(dve_c, done[0])
            v.tensor_scalar(se_r[:, :], se_sq[:, :], 1.0 / D, None, ALU.mult).then_inc(se_sum, 1)

            dve.wait_ge(aal_up, 1)
            for n in range(ND):
                dve.wait_ge(dist_ps, n + 1)
                rows = cost[:, 1 + DG * n:1 + DG * n + DG, 1:R]
                link(v.tensor_tensor(rows, bank(n % 3)[:, 0:DG * N].rearrange("p (s n) -> p s n", n=N),
                                     aa_l[:, None, :].to_broadcast([P, DG, N]), ALU.add))
                v.tensor_scalar(rows, rows, 0.0, None, ALU.max).then_inc(dist2_up, 1)

            dve.wait_ge(se_root, 1)
            link(v.tensor_scalar(se_r[:, :], se_r[:, :], RMS_EPS / D ** 0.5, None, ALU.max))
            link(v.reciprocal(se_r[:, :], se_r[:, :]))
            for k in range(KS):
                v.tensor_scalar(se_n[:, k, :], se_n[:, k, :], se_r[:, k:k + 1], None, ALU.mult).then_inc(se_up, 1)

            from_above = [i if i % LPB == 0 else i - 1 for i in range(32)]
            marked = [0]

            def flag_left(s):
                v.tensor_tensor(left_f[:, s, :], cost[:, s, 1:R], cost[:, s + 1, 0:N], ALU.is_lt).then_inc(flags_up, 1)

            def flag_diag(s):
                v.tensor_tensor(diag_f[:, s, :], cost[:, s, 0:N], cost[:, s + 1, 0:N], ALU.is_le).then_inc(flags_d, 1)

            for s in range(STEPS):
                if s >= 1:
                    dve.wait_ge(wave_r, s)
                v.stream_shuffle(cost[:, s + 1, 0:1], cost[:, s, N:R], from_above).then_inc(wave_b, 1)
                v.tensor_tensor(m_s[:, s % 2, :], cost[:, s, 1:R], cost[:, s, 0:N], ALU.min).then_inc(wave_m, 1)
                if s >= 1:
                    flag_left(s - 1)
                if s % DG == 0:
                    dve.wait_ge(dist_up, s // DG + 1)
                dve.wait_ge(wave_b, s + 1)
                dve.wait_ge(wave_m, s + 1)
                v.tensor_tensor_scan(cost[:, s + 1, 1:R], m_s[:, s % 2, :], cost[:, s + 1, 1:R],
                                     cost[:, s + 1, 0:1], ALU.min, ALU.add).then_inc(wave_r, 1)
                if s >= 1:
                    flag_diag(s - 1)
            dve.wait_ge(wave_r, STEPS)
            flag_left(STEPS - 1)
            flag_diag(STEPS - 1)

            from_below = [i if i % LPB == 0 else (i + 1) % 32 for i in range(32)]

            def merge_flags(s):
                dve.wait_ge(flags_up, s + 1)
                dve.wait_ge(flags_d, s + 1)
                v.tensor_tensor(left_f[:, s, :], left_f[:, s, :], diag_f[:, s, :], ALU.max).then_inc(merge_up, 1)

            def pick_keys(s):
                dve.wait_ge(key_up, s // DG + 1)
                dve.wait_ge(merge_up, STEPS - s)
                v.tensor_tensor(key_t[:, s, :], left_f[:, s, :], key_t[:, s, :], ALU.mult).then_inc(pick_up, 1)

            last = STEPS - 1
            dve.wait_ge(flags_up, STEPS)
            dve.wait_ge(flags_d, STEPS)
            merge_flags(last)
            merge_flags(last - 1)
            pick_keys(last)
            for s in range(last, -1, -1):
                i = last - s
                dve.wait_ge(keys_up, i + 1)
                v.stream_shuffle(hit[:, i % 2, 0:1], keys[:, s + 1:s + 2], from_below).then_inc(hit_b, 1)
                dve.wait_ge(pick_up, i + 1)
                v.scalar_tensor_tensor(hit[:, i % 2, 1:R], key4[:, :], keys[:, s + 1:s + 2], key_t[:, s, :],
                                       ALU.is_lt, ALU.mult).then_inc(hit_up, 1)
                if s >= 2:
                    merge_flags(s - 2)
                dve.wait_ge(hit_b, i + 1)
                dve.wait_ge(hit_up, i + 1)
                v.reduce_max(keys[:, s:s + 1], hit[:, i % 2, :], AX.X).then_inc(keys_up, 1)
                if s >= 1:
                    pick_keys(s - 1)

            dve.wait_ge(kb_ps, 1)
            v.memset(mask[0:N, :, :, S:SP], 0.0).then_inc(dve_c, 1)
            done[0] += 1
            link(v.tensor_copy(keys_b[0:N, :, :], bank(0)[0:N, 0:B * (S + 1)].rearrange("p (b s) -> p b s", b=B)))
            for c in range(C):
                if c >= 2:
                    dve.wait_ge(mask_up, c - 1)
                v.tensor_scalar(under[0:N, c % 2, :, :], keys_b[0:N, :, 1:S + 1], row4[0:N, c:c + 1], None,
                                ALU.is_gt).then_inc(under_up, 1)
                if c >= 1:
                    dve.wait_ge(under_up, c)
                    v.scalar_tensor_tensor(mask[0:N, c - 1, :, 0:S], keys_b[0:N, :, 0:S], row4b[0:N, c - 1:c],
                                           under[0:N, (c - 1) % 2, :, :], ALU.is_lt, ALU.mult).then_inc(mask_up, 1)
            dve.wait_ge(under_up, C)
            v.scalar_tensor_tensor(mask[0:N, C - 1, :, 0:S], keys_b[0:N, :, 0:S], row4b[0:N, C - 1:C],
                                   under[0:N, (C - 1) % 2, :, :], ALU.is_lt, ALU.mult).then_inc(mask_up, 1)
            link(v.tensor_reduce(csum[:, :], csum_g[:, :, :], AX.X, ALU.add))
            link(v.tensor_scalar(csum[:, :], csum[:, :], 1.0 / L, None, ALU.mult))
            v.tensor_copy(csum_b[:, :, :], csum[:, :, None].to_broadcast([P, B, SP])).then_inc(csum_up, 1)
            link(v.tensor_copy(rtemp[:, :], temp_s[:, :]))
            link(v.reciprocal(rtemp[:, :], rtemp[:, :]))

            dve.wait_ge(exp_ps, 1)
            dve.wait_ge(tg_up, 2)
            for h in range(2):
                rows = slice(SP * h, SP * h + SP)
                mark(v.scalar_tensor_tensor(x_s[rows, :, :], ps[rows, 1:1 + TT, h * D:(h + 1) * D], tgx[rows, 0:1],
                                            x_s[rows, :, :], ALU.mult, ALU.add))
            dve.wait_ge(dve_c, done[0])
            row_stats()
            mark(v.tensor_copy(vv[:, 0, :], mv[:, :, 1]))
            v.tensor_scalar(vv[:, 1, :], mv[:, :, 1], LN_EPS, None, ALU.add).then_inc(var_up, 1)
            dve.wait_ge(pool_pow, 2)
            link(v.scalar_tensor_tensor(den[:, :], vr[:, 1, :], RMS_EPS / D ** 0.5, vr[:, 0, :], ALU.mult, ALU.max))
            link(v.reciprocal(fac[:, :], den[:, :]))
            for t in range(TT):
                v.tensor_scalar(xn_s[:, t, :], x_s[:, t, :], mv[:, t, 0:1], fac[:, t:t + 1],
                                ALU.subtract, ALU.mult).then_inc(xn_up, 1)
            for k in range(KS):
                dve.wait_ge(ld_ps, k + 1)
                logits = bank(4 + k)[:, 0:B * S].rearrange("p (b s) -> p b s", b=B)
                link(v.reduce_max(d_max[:, k, :], logits, AX.X))
                v.tensor_tensor(disp_e[:, k, :, 0:S], logits, d_max[:, k, :, None].to_broadcast([P, B, S]),
                                ALU.subtract).then_inc(ld_sub, 1)
            for t in range(TT):
                dve.wait_ge(lc_ps, t + 1)
                v.tensor_reduce(c_nmax[:, t:t + 1], bank(t), AX.X, ALU.max, negate=True).then_inc(lc_max, 1)
            for k in range(KS):
                dve.wait_ge(ld_exp, k + 1)
                mark(v.tensor_reduce(d_sum[:, k, :], disp_e[:, k, :, 0:S], AX.X, ALU.add))
            dve.wait_ge(dve_c, done[0])
            v.reciprocal(d_inv[:, :, :], d_sum[:, :, :]).then_inc(d_inv_up, 1)
            for k in range(KS):
                dve.wait_ge(comb_ps, k + 1)
                v.tensor_copy(comb_t[:, k, :], bank(k)).then_inc(comb_up, 1)
            dve.wait_ge(lc_exp, TT)
            link(v.reciprocal(c_inv[:, :], c_sum[:, :]))
            link(v.tensor_scalar(tgr[:, :], c_inv[:, :], tgf[:, 0:1], None, ALU.mult))
            for b in range(B):
                dve.wait_ge(hy_used, KS * (b + 1))
                v.tensor_copy(y_t[:, :, SP * b:SP * b + S],
                              bank(b % 2)[:, 0:Q * S].rearrange("p (q s) -> p q s", q=Q)).then_inc(y_up, 1)
            for t in range(TT):
                dve.wait_ge(f0_ps, TT)
                mark(v.scalar_tensor_tensor(x_s[:, t, :], bank(2)[:, t * D:(t + 1) * D], tgr[:, t:t + 1], x_s[:, t, :],
                                            ALU.mult, ALU.add))
            dve.wait_ge(dve_c, done[0])
            layer_norm(3)
            for t in range(TT):
                dve.wait_ge(xa_ps, TT)
                mark(v.scalar_tensor_tensor(x_s[:, t, :], bank(4)[:, t * D:(t + 1) * D], tgx[:, 1:2], x_s[:, t, :],
                                            ALU.mult, ALU.add))
            dve.wait_ge(dve_c, done[0])
            layer_norm(4)
            dve.wait_ge(g_ps, 1)
            link(v.tensor_scalar(gates[:, :, :].rearrange("p t e -> p (t e)"), bank(6)[:, 0:TT * E], rtemp[:, 0:1],
                                 None, ALU.mult))
            for t in range(TT):
                mark(v.max(top[:, t, :], gates[:, t, :]))
            dve.wait_ge(dve_c, done[0])
            v.tensor_tensor(gdiff[:, :], top[:, :, 1], top[:, :, 0], ALU.subtract).then_inc(gd_up, 1)
            for t in range(TT):
                mark(v.max_index(top_i[:, t, :], top[:, t, :], gates[:, t, :]))
            dve.wait_ge(dve_c, done[0])
            mark(v.tensor_copy(top_f[:, :, :], top_i[:, :, 0:2]))
            dve.wait_ge(ge_up, 1)
            link(v.tensor_scalar(gden[:, :], gexp[:, :], 1.0, None, ALU.add))
            link(v.reciprocal(wgt[:, 0, :], gden[:, :]))
            link(v.tensor_tensor(wgt[:, 1, :], wgt[:, 0, :], gexp[:, :], ALU.mult))
            for t in range(TT):
                for j, dst in ((0, wt1), (1, wt2)):
                    mark(v.tensor_scalar(dst[:, t, :], e_iota[:, :], top_f[:, t, j:j + 1], wgt[:, j, t:t + 1],
                                         ALU.is_equal, ALU.mult))
            dve.wait_ge(dve_c, done[0])
            v.tensor_tensor(wt[:, :, :], wt1[:, :, :], wt2[:, :, :], ALU.add).then_inc(wt_up, 1)
            dve.wait_ge(wtt_ps, 1)
            v.tensor_copy(wt_t[:, :], bank(7)[0:E, :]).then_inc(wtt_up, 1)
            dve.wait_ge(b2_ps, 1)
            v.tensor_copy(acc[:, :, :].rearrange("p t d -> p (t d)"), bank(3)).then_inc(acc_up, 1)
            for e in range(E):
                dve.wait_ge(eo_ps, e + 1)
                for t in range(TT):
                    dve.wait_ge(acc_up, 1) if e == 0 else dve.wait_ge(eo_up, TT * (e - 1) + t + 1)
                    v.scalar_tensor_tensor(acc[:, t, :], bank(4 + e % 2)[:, t * D:(t + 1) * D], wt[:, t, e:e + 1],
                                           acc[:, t, :], ALU.mult, ALU.add).then_inc(eo_up, 1)
            for t in range(TT):
                dve.wait_ge(eo_up, TT * (E - 1) + t + 1)
                v.scalar_tensor_tensor(x_s[:, t, :], acc[:, t, :], tgf[:, 1:2], x_s[:, t, :],
                                       ALU.mult, ALU.add).then_inc(fin_up, 1)


_INS = ['x', 'ctx_1024', 'g_xattn', 'g_ffn', 'L0_ffn_gamma_x', 'L0_ffn_gamma_slot', 'L0_ffn_slot_embeds',
        'L0_ffn_w1', 'L0_ffn_w2', 'L1_xattn_W', 'L1_xattn_b', 'L1_ffn_W1', 'L1_ffn_b1', 'L1_ffn_W2', 'L1_ffn_b2',
        'L1_ffn_gate_w', 'L1_ffn_gate_b', 'L1_ffn_temperature']


def kernel(**inputs):
    import numpy as _np
    import concourse.bacc as _bacc
    from concourse import mybir as _mybir
    from concourse.bass_utils import run_bass_kernel_spmd as _run

    nc = _bacc.Bacc("TRN2", target_bir_lowering=False, num_devices=1)
    arrays, args = {}, []
    for name in _INS:
        a = _np.ascontiguousarray(inputs[name])
        if a.ndim == 0:
            a = a.reshape(1)
        arrays[f"in_{name}_dram"] = a
        args.append(nc.dram_tensor(f"in_{name}_dram", a.shape, _mybir.dt.from_np(a.dtype), kind="ExternalInput").ap())
    shape = inputs['x'].shape
    out = nc.dram_tensor("out_0_dram", tuple(shape), _mybir.dt.float32, kind="ExternalOutput").ap()
    gated_stack(nc, *args, out)
    r = _run(nc, [arrays], core_ids=[0])
    return r.results[0]["out_0_dram"]
```

```python
from contextlib import ExitStack

import concourse.bass as bass
from concourse import mybir

F32 = mybir.dt.float32
BF16 = mybir.dt.bfloat16
I32 = mybir.dt.int32
ALU = mybir.AluOpType
ACT = mybir.ActivationFunctionType
AX = mybir.AxisListType

P = 128
LN_EPS = 1e-5
RMS_EPS = 1e-12
TINY = 1e-37
INF = 1e30
PAD_D2 = 1e35


def gated_stack(nc, x, ctx_in, g_xattn, g_ffn, gamma_x, gamma_slot, slot_embeds, w1, w2, Wc, bc,
                eW1, eb1, eW2, eb2, gate_w, gate_b, temperature, out):
    B, S, D = x.shape
    L = ctx_in.shape[1]
    LPB = P // B
    C = LPB - 1
    N = L // C
    R = N + 1
    STEPS = S + C - 1
    TT = B // 2
    SP = P // 2
    NS, NT, _ = slot_embeds.shape
    SLOTS = NS * NT
    KS = SLOTS // P
    HID = w1.shape[1]
    Q = HID // P
    E = eW1.shape[0]
    assert D == P and C * N == L and B * LPB == P and S <= SP
    LAST_KEY = 4 * L + 8
    assert 4 * L * 2.0 ** -12 < 2
    TG = 5
    GPB = C // TG
    NG = B * GPB
    HALVES = ((0, 8), (8, C))
    DG = 5
    ND = STEPS // DG
    SPANS = [(DG * n, DG * n + DG) for n in range(ND - 1)] + [(STEPS - DG, STEPS - 2), (STEPS - 2, STEPS)]
    NSP = len(SPANS)
    NMERGE = 3
    AHEAD_S = SPANS[NSP - NMERGE][0]
    SMALL_AT = 2
    SIDE = 2.0 ** -12
    KEYS_A = 14
    WARM_AT = 8
    KEYS_WARM, MASK_WARM, NORM_WARM = 20, 10, 24
    START_WARM = 30
    ACT_SQ = 5
    POOL_SQ = 8

    with ExitStack() as stack:
        def sb(name, shape, dt=F32):
            return stack.enter_context(nc.sbuf_tensor(name, shape, dt))

        def sem(name):
            return stack.enter_context(nc.semaphore(name))

        ctx_n = sb("ctx_n", [P, B * C, D])
        region_x = sb("region_x", [P, B * L])
        ctx_t = region_x[:, :].rearrange("p (g n) -> p g n", n=N)
        key_t = region_x[:, 0:STEPS * R].rearrange("p (s n) -> p s n", n=R)
        ew1_s = region_x[:, 7072:7072 + E * HID].rearrange("p (e f) -> p e f", e=E)
        disp_e = region_x[:, 0:KS * B * SP].rearrange("p (k b s) -> p k b s", k=KS, b=B)
        comb_e = region_x[:, 2048:2048 + TT * SLOTS].rearrange("p (t n) -> p t n", t=TT)
        xw_s = region_x[:, 4096:4096 + TT * HID].rearrange("p (t f) -> p t f", t=TT)
        ht_s = region_x[:, 0:2 * Q * B * SP].rearrange("p (r q n) -> p r q n", r=2, q=Q)
        region_d = sb("region_d", [P, STEPS * P])
        prod = region_d[:, :].rearrange("p (s l) -> p s l", l=P)
        flags = region_d[:, :].bitcast(BF16).rearrange("p (s n) -> p s n", n=2 * P)
        left_f = flags[:, :, 0:N]
        diag_f = flags[:, :, N:2 * N]
        mask = region_d[:, 0:C * B * SP].rearrange("p (c b s) -> p c b s", c=C, b=B)
        under = region_d[:, 7680:7680 + 2 * B * S].rearrange("p (r b s) -> p r b s", r=2, b=B)
        acc = region_d[:, 0:TT * D].rearrange("p (t d) -> p t d", t=TT)
        wt_t = region_d[0:E, 512:512 + TT * P]
        disp_t = region_d[:, 0:TT * SLOTS].rearrange("p (t n) -> p t n", t=TT)
        comb_t = region_d[:, 2048:2048 + KS * B * SP].rearrange("p (k n) -> p k n", k=KS)
        NHR = 4
        h_s = region_d[:, 4096:4096 + NHR * HID].rearrange("p (r f) -> p r f", r=NHR)
        y_t = region_d[:, 6144:6144 + Q * B * SP].rearrange("p (q n) -> p q n", q=Q)
        region_w = sb("region_w", [P, (STEPS + 1) * R])
        cost = region_w[:, :].rearrange("p (s r) -> p s r", r=R)
        squares = region_w[:, 1024:1024 + 2 * POOL_SQ * D].rearrange("p (r c d) -> p r c d", r=2, d=D)
        ew2_s = region_w[:, 0:E * HID].rearrange("p (e q d) -> p e q d", e=E, q=Q)

        x_s = sb("x_s", [P, TT, D])
        xn_s = sb("xn_s", [P, TT, D])
        xt_s = sb("xt_s", [P, B * SP])
        xsq_s = sb("xsq_s", [P, B * SP])
        hit = xsq_s[:, 0:2 * R].rearrange("p (r n) -> p r n", n=R)
        below = xsq_s[:, 2 * R:4 * R].rearrange("p (r n) -> p r n", n=R)
        bb_s = sb("bb_s", [P, B, SP])
        stats = sb("stats", [P, TT, 6])
        mv = sb("mv", [P, TT, 2])
        vv = sb("vv", [P, 2, TT])
        vr = sb("vr", [P, 2, TT])
        den = sb("den", [P, TT])
        fac = sb("fac", [P, TT])
        half = sb("half", [P, 2 * TT])
        mhalf = sb("mhalf", [P, TT])
        ident = sb("ident", [P, P])
        ones = sb("ones", [P, P])
        aa_n = sb("aa_n", [P, P])
        turn = sb("turn", [P, N])
        junk_v = sb("junk_v", [P, 2, D])
        junk_a = sb("junk_a", [P, 2, D])
        lane_i = sb("lane_i", [P, 1], I32)
        lane_m = sb("lane_m", [P, 1], I32)
        lane_f = sb("lane_f", [P, 1])
        lane4 = sb("lane4", [P, 1])
        tiny = sb("tiny", [P, 1])
        lane0 = sb("lane0", [P, 1])
        key_row = sb("key_row", [P, N])
        key4 = sb("key4", [P, N])
        m_s = sb("m_s", [P, 2, N])
        keys = sb("keys", [P, STEPS + 1])
        lane_sel = sb("lane_sel", [P, B])
        keys_x = sb("keys_x", [P, B, S + 1])
        row4 = sb("row4", [P, C])
        row4b = sb("row4b", [P, C])
        csum_g = sb("csum_g", [P, B, GPB])
        csum = sb("csum", [P, B])
        csum_b = sb("csum_b", [P, B, SP])
        gx_b = sb("gx_b", [P, 2])
        gf_b = sb("gf_b", [P, 2])
        tgx = sb("tgx", [P, 2])
        tgf = sb("tgf", [P, 2])
        tgr = sb("tgr", [P, TT])
        gam_x = sb("gam_x", [P, 1])
        gam_s = sb("gam_s", [P, 1])
        se_n = sb("se_n", [P, KS, D])
        se_sq = sb("se_sq", [P, KS])
        se_r = sb("se_r", [P, KS])
        se_t = sb("se_t", [P, SLOTS])
        w1_s = sb("w1_s", [P, HID])
        w2_s = sb("w2_s", [P, Q, D])
        wc_n = sb("wc_n", [P, 2, D])
        wc_t = sb("wc_t", [P, 2, D])
        bc_s = sb("bc_s", [1, D])
        b1_n = sb("b1_n", [E * Q, P])
        b1_t = sb("b1_t", [P, E * Q])
        b2_s = sb("b2_s", [E, D])
        gw_s = sb("gw_s", [P, E])
        gb_s = sb("gb_s", [1, E])
        temp_s = sb("temp_s", [P, 1])
        rtemp = sb("rtemp", [P, 1])
        d_max = sb("d_max", [P, KS, B])
        d_sum = sb("d_sum", [P, KS, B])
        d_inv = sb("d_inv", [P, KS, B])
        c_nmax = sb("c_nmax", [P, TT])
        c_sum = sb("c_sum", [P, TT])
        c_inv = sb("c_inv", [P, TT])
        gates = sb("gates", [P, TT, E])
        top = sb("top", [P, TT, 8])
        top_i = sb("top_i", [P, TT, 8], mybir.dt.uint32)
        top_f = sb("top_f", [P, TT, 2])
        e_iota = sb("e_iota", [P, E])
        gdiff = sb("gdiff", [P, TT])
        gexp = sb("gexp", [P, TT])
        gden = sb("gden", [P, TT])
        wgt = sb("wgt", [P, 2, TT])
        wt1 = sb("wt1", [P, TT, E])
        wt2 = sb("wt2", [P, TT, E])
        wt = sb("wt", [P, TT, E])

        ps = stack.enter_context(nc.psum_tensor("ps", [P, 8, 512], F32))

        x_in = sem("x_in")
        small_in = sem("small_in")
        ctx_part = [sem(f"ctx_in{b}") for b in range(B)]
        ew1_in = sem("ew1_in")
        ew2_in = sem("ew2_in")
        out_done = sem("out_done")
        zeroed = sem("zeroed")
        consts = sem("consts")
        pads = sem("pads")
        pool_pow = sem("pool_pow")
        var_up = sem("var_up")
        dve_c = sem("dve_c")
        xn_up = sem("xn_up")
        xt_ps = sem("xt_ps")
        xt_up = sem("xt_up")
        bb_ps = sem("bb_ps")
        bb_up = sem("bb_up")
        small_ps = sem("small_ps")
        small_up = sem("small_up")
        se_up = sem("se_up")
        ctx_ps = sem("ctx_ps")
        ctx_up = sem("ctx_up")
        prod_ps = sem("prod_ps")
        prod_up = sem("prod_up")
        aa_up = sem("aa_up")
        bb_rows = sem("bb_rows")
        dist_ps = sem("dist_ps")
        dist_up = sem("dist_up")
        wave_m = sem("wave_m")
        wave_r = sem("wave_r")
        flags_up = sem("flags_up")
        gap_up = sem("gap_up")
        sign_up = sem("sign_up")
        key_up = sem("key_up")
        scaled_up = sem("scaled_up")
        picked_up = sem("picked_up")
        below_up = sem("below_up")
        keys_up = sem("keys_up")
        keys_a = sem("keys_a")
        keys_z = sem("keys_z")
        kb_ps = sem("kb_ps")
        mask_up = sem("mask_up")
        exp_ps = sem("exp_ps")
        csum_up = sem("csum_up")
        tg_up = sem("tg_up")
        xw_ps = sem("xw_ps")
        xw_up = sem("xw_up")
        ld_ps = sem("ld_ps")
        ld_sub = sem("ld_sub")
        ld_exp = sem("ld_exp")
        lc_ps = sem("lc_ps")
        lc_max = sem("lc_max")
        lc_exp = sem("lc_exp")
        d_inv_up = sem("d_inv_up")
        disp_ps = sem("disp_ps")
        disp_up = sem("disp_up")
        comb_ps = sem("comb_ps")
        comb_up = sem("comb_up")
        h_ps = sem("h_ps")
        h_up = sem("h_up")
        y_up = sem("y_up")
        hy_used = sem("hy_used")
        f0_ps = sem("f0_ps")
        xa_ps = sem("xa_ps")
        g_ps = sem("g_ps")
        gd_up = sem("gd_up")
        ge_up = sem("ge_up")
        wt_up = sem("wt_up")
        wtt_ps = sem("wtt_ps")
        wtt_up = sem("wtt_up")
        b2_ps = sem("b2_ps")
        eh_ps = sem("eh_ps")
        eh_up = sem("eh_up")
        eo_ps = sem("eo_ps")
        eo_up = sem("eo_up")
        fin_up = sem("fin_up")
        pads2 = sem("pads2")
        aa_pool = sem("aa_pool")
        sq_up = sem("sq_up")
        aa_act = sem("aa_act")
        gap2_up = sem("gap2_up")
        flags_d = sem("flags_d")
        merge_up = sem("merge_up")
        under_up = sem("under_up")
        acc_up = sem("acc_up")
        se_sum = sem("se_sum")
        se_root = sem("se_root")
        g_in = sem("g_in")
        se_in = sem("se_in")
        w12_in = sem("w12_in")
        relu_up = sem("relu_up")

        def bank(i):
            return ps[:, i, :]

        keys_b = bank(0)[:, 0:B * (S + 1)].rearrange("p (b s) -> p b s", b=B)

        def tokens(ap):
            return ap.rearrange("p (b s) -> p b s", b=B)[:, :, 0:S]

        def lane(b, c):
            return LPB * b + 1 + c

        QUARTER = N // 32 * 32

        def diagonal(b, c0, c1, row0, row1):
            base = prod[row0:row1, c0, lane(b, c0):lane(b, c0) + 1]
            return bass.AP(tensor=base.tensor, offset=base.offset,
                           ap=[list(base.ap[0]), [P + 1, c1 - c0], [P, S]])

        SMALL_ALL = 16 * 9
        CONSTS = 7
        SIGN_LAG = 3
        block = stack.enter_context(nc.Block())

        @block.sync
        def _(sp):
            sp.wait_ge(zeroed, 1)
            for h in range(2):
                sp.dma_start(x_s[SP * h:SP * h + S, :, :],
                             x[h::2, :, :].rearrange("t s d -> s t d")).then_inc(x_in, 16)
            for b in range(B):
                src = ctx_in[b, :, :].rearrange("(c p) d -> p c d", p=N)
                for p0, p1 in ((0, 96), (96, N)):
                    sp.dma_start(ctx_n[p0:p1, C * b:C * b + C, :], src[p0:p1, :, :]).then_inc(ctx_part[b], 16)
            sp.dma_start(w1_s[:, :], w1).then_inc(w12_in, 16)
            sp.dma_start(w2_s[:, :, :], w2.rearrange("(q p) d -> p q d", p=P)).then_inc(w12_in, 16)
            sp.wait_ge(prod_ps, 2 * B)
            sp.dma_start(ew1_s, eW1.rearrange("e d f -> d e f")).then_inc(ew1_in, 16)
            sp.wait_ge(flags_up, 2 * STEPS)
            sp.wait_ge(gap2_up, NSP)
            sp.dma_start(ew2_s, eW2.rearrange("e (q p) d -> p e q d", p=P)).then_inc(ew2_in, 16)
            for t in range(TT):
                sp.wait_ge(fin_up, t + 1)
                for h in range(2):
                    sp.dma_start(out[2 * t + h, :, :], x_s[SP * h:SP * h + S, t, :]).then_inc(out_done, 16)
            sp.wait_ge(out_done, 16 * 2 * TT)

        @block.gpsimd
        def _(pool):
            g = nc.gpsimd
            g.memset(ident[:, :], 0.0).then_inc(consts, 1)
            g.memset(ones[:, :], 1.0).then_inc(consts, 1)
            pool.wait_ge(consts, 2)
            g.affine_select(out=ident[:, :], in_=ident[:, :], compare_op=ALU.not_equal, fill=1.0, base=0,
                            pattern=[[-1, P]], channel_multiplier=1).then_inc(consts, 1)
            g.memset(half[:, :], 0.5).then_inc(consts, 1)
            g.memset(mhalf[:, :], -0.5).then_inc(consts, 1)
            g.iota(lane_i[:, :], pattern=[[0, 1]], base=0, channel_multiplier=1).then_inc(consts, 1)
            g.iota(key_row[:, :], pattern=[[4, N]], base=4 - 4 * N, channel_multiplier=0,
                   allow_small_or_imprecise_dtypes=True).then_inc(consts, 1)
            pool.wait_ge(var_up, 1)
            g.tensor_tensor(vr[:, 0, :], vv[:, 1, :], mhalf[:, :], ALU.pow).then_inc(pool_pow, 1)
            g.memset(prod[:, 0:C - 1, :], PAD_D2).then_inc(pads, 1)
            g.memset(prod[:, S:STEPS, :], PAD_D2).then_inc(pads, 1)
            g.memset(prod[:, C - 1:S, 0:P:LPB], PAD_D2).then_inc(pads, 1)
            g.memset(turn[:, :], 0.0).then_inc(pads, 1)
            g.memset(tiny[:, :], TINY).then_inc(pads2, 1)
            g.memset(lane_sel[:, :], 0.0).then_inc(pads, 1)
            pool.wait_ge(pads, 5)
            g.affine_select(out=turn[:, :], in_=turn[:, :], compare_op=ALU.not_equal, fill=1.0, base=0,
                            pattern=[[-1, N]], channel_multiplier=1).then_inc(pads, 1)
            pool.wait_ge(pads, 6)
            g.affine_select(out=turn[:, :], in_=turn[:, :], compare_op=ALU.not_equal, fill=1.0, base=-N,
                            pattern=[[0, N]], channel_multiplier=1).then_inc(pads, 1)
            g.affine_select(out=lane_sel[:, :], in_=lane_sel[:, :], compare_op=ALU.not_equal, fill=1.0,
                            base=-1, pattern=[[-LPB, B]], channel_multiplier=1).then_inc(pads2, 1)
            g.iota(row4[:, :], pattern=[[4 * N, C]], base=4, channel_multiplier=4,
                   allow_small_or_imprecise_dtypes=True).then_inc(pads2, 1)
            g.iota(row4b[:, :], pattern=[[4 * N, C]], base=6, channel_multiplier=4,
                   allow_small_or_imprecise_dtypes=True).then_inc(pads2, 1)
            g.iota(e_iota[:, :], pattern=[[1, E]], base=0, channel_multiplier=0,
                   allow_small_or_imprecise_dtypes=True).then_inc(pads2, 1)
            for b in range(B):
                pool.wait_ge(ctx_part[b], 32)
                if b >= 2:
                    pool.wait_ge(aa_pool, b - 1)
                if b >= 1:
                    pool.wait_ge(sq_up, b)
                rows = ctx_n[0:N, C * b + ACT_SQ:C * b + ACT_SQ + POOL_SQ, :]
                g.tensor_tensor(squares[0:N, b % 2, :, :], rows, rows, ALU.mult).then_inc(sq_up, 1)
            pool.wait_ge(prod_ps, 2 * B)
            for s0, s1 in SPANS:
                rows = cost[:, s0:s1, :]
                pool.wait_ge(wave_r, s1 - 1)
                g.tensor_tensor(key_t[:, s0:s1, 1:R], rows[:, :, 0:N], rows[:, :, 1:R],
                                ALU.subtract).then_inc(gap_up, 1)
                pool.wait_ge(wave_r, s1)
                g.tensor_tensor(diag_f[:, s0:s1, :], cost[:, s0 + 1:s1 + 1, 0:N], rows[:, :, 0:N],
                                ALU.subtract).then_inc(gap2_up, 1)
            pool.wait_ge(key_up, NSP)
            for n in range(NSP - 2, -1, -1):
                s0, s1 = SPANS[n]
                rows = key_t[:, s0:s1, 1:R]
                g.tensor_tensor(rows, rows, key4[:, None, :].to_broadcast([P, s1 - s0, N]),
                                ALU.mult).then_inc(scaled_up, 1)
                pool.wait_ge(scaled_up, NSP - 1 - n)
                pool.wait_ge(merge_up, NMERGE + max(0, AHEAD_S - s0))
                g.tensor_tensor(rows, rows, left_f[:, s0:s1, :], ALU.mult).then_inc(picked_up, 1)
            pool.wait_ge(picked_up, NSP - 1)
            g.memset(mask[0:N, :, :, S:SP], 0.0).then_inc(pads2, 1)
            for n in range(1, 4):
                pool.wait_ge(var_up, n + 1)
                if n == 1:
                    g.tensor_tensor(vr[:, :, :].rearrange("p a t -> p (a t)"),
                                    vv[:, :, :].rearrange("p a t -> p (a t)"), half[:, :], ALU.pow).then_inc(pool_pow, 1)
                else:
                    g.tensor_tensor(vr[:, 0, :], vv[:, 1, :], mhalf[:, :], ALU.pow).then_inc(pool_pow, 1)
                if n == 1:
                    pool.wait_ge(exp_ps, 1)
                    g.memset(disp_e[:, :, :, S:SP], 0.0).then_inc(pads2, 1)
                    g.memset(y_t.rearrange("p q (b s) -> p q b s", b=B)[:, :, :, S:SP], 0.0).then_inc(pads2, 1)
                if n == 2:
                    pool.wait_ge(hy_used, B * KS)
                    g.memset(ht_s.rearrange("p r q (b s) -> p (r q b) s", b=B)[:, :, S:SP], 0.0).then_inc(pads2, 1)

        @block.scalar
        def _(act):
            a = nc.scalar
            act.dma_start(gx_b[:, :], g_xattn.unsqueeze(0).to_broadcast([P, 2])).then_inc(g_in, 16)
            act.dma_start(gf_b[:, :], g_ffn.unsqueeze(0).to_broadcast([P, 2])).then_inc(g_in, 16)
            act.dma_start(se_n[:, :, :], slot_embeds.rearrange("e t d -> (e t) d").rearrange("(k p) d -> p k d", p=P))\
               .then_inc(se_in, 16)
            for dst, src in (
                (wc_n[:, :, :], Wc.rearrange("e (h d) -> e h d", h=2)),
                (b1_n[:, :], eb1.rearrange("e (q p) -> (e q) p", p=P)),
                (gam_x[:, :], gamma_x.unsqueeze(1)),
                (gam_s[:, :], gamma_slot.unsqueeze(1)),
                (bc_s[:, :], bc.unsqueeze(0)),
                (b2_s[:, :], eb2),
                (gw_s[:, :], gate_w),
                (gb_s[:, :], gate_b.unsqueeze(0)),
                (temp_s[:, :], temperature.unsqueeze(0).to_broadcast([P, 1])),
            ):
                act.dma_start(dst, src).then_inc(small_in, 16)
            act.wait_ge(g_in, 32)
            a.activation(tgx[:, :], gx_b[:, :], ACT.Tanh).then_inc(tg_up, 1)
            a.activation(tgf[:, :], gf_b[:, :], ACT.Tanh).then_inc(tg_up, 1)
            act.wait_ge(se_sum, 1)
            a.activation(se_r[:, :], se_r[:, :], ACT.Sqrt).then_inc(se_root, 1)
            act.wait_ge(xt_ps, 1)
            a.activation(xt_s[:, :], bank(6), ACT.Copy, scale=-2.0).then_inc(xt_up, 1)
            a.activation(xsq_s[:, :], bank(6), ACT.Square).then_inc(xt_up, 1)
            act.wait_ge(bb_ps, 1)
            a.activation(bb_s[:, :, :].rearrange("p b s -> p (b s)"), bank(6), ACT.Copy).then_inc(bb_up, 1)

            nsq = [0]
            for k in range(NG):
                act.wait_ge(ctx_ps, k + 1)
                a.activation(region_x[:, k * TG * N:(k + 1) * TG * N], bank(k % 3)[:, 0:TG * N], ACT.Copy,
                             accum_out=csum_g[:, k // GPB, k % GPB:k % GPB + 1]).then_inc(ctx_up, 1)
                b = k // GPB
                for c in range(k % GPB, ACT_SQ, GPB):
                    if nsq[0] >= 2:
                        act.wait_ge(aa_act, nsq[0] - 1)
                    a.activation(junk_a[0:N, nsq[0] % 2, :], ctx_n[0:N, C * b + c, :], ACT.Square,
                                 accum_out=aa_n[0:N, lane(b, c):lane(b, c) + 1]).then_inc(aa_act, 1)
                    nsq[0] += 1
            act.wait_ge(pads2, 5)
            for n in range(SIGN_LAG + NSP):
                if n < ND:
                    act.wait_ge(dist_ps, n + 1)
                    if n == 0:
                        act.wait_ge(aa_pool, B)
                    rows = cost[:, 1 + DG * n:1 + DG * n + DG, 1:R]
                    a.activation(rows, bank(n % 3)[:, 0:DG * N].rearrange("p (s n) -> p s n", n=N),
                                 ACT.Relu).then_inc(relu_up, 1)
                    act.wait_ge(relu_up, n + 1)
                    a.activation(rows, rows, ACT.Sqrt).then_inc(dist_up, 1)
                if n >= SIGN_LAG:
                    m = n - SIGN_LAG
                    s0, s1 = SPANS[m]
                    act.wait_ge(gap_up, m + 1)
                    rows = key_t[:, s0:s1, 1:R]
                    a.activation(rows, rows, ACT.Sign).then_inc(sign_up, 1)
                    act.wait_ge(sign_up, m + 1)
                    a.activation(rows, rows, ACT.Copy, scale=SIDE, bias=1.0).then_inc(key_up, 1)
                    act.wait_ge(gap2_up, m + 1)
                    rows = diag_f[:, s0:s1, :]
                    a.activation(rows, rows, ACT.Sign, bias=tiny[:, 0:1]).then_inc(flags_d, 1)
                if n == SMALL_AT:
                    act.wait_ge(small_ps, 1)
                    a.activation(wc_t[:, :, :].rearrange("p h d -> p (h d)"), bank(7)[:, 0:2 * D], ACT.Copy).then_inc(small_up, 1)
                    a.activation(b1_t[:, :], bank(7)[:, 2 * D:2 * D + E * Q], ACT.Copy).then_inc(small_up, 1)
                    act.wait_ge(small_ps, 2)
                    a.activation(se_t[:, :], bank(5), ACT.Copy, scale=gam_s[:, 0:1]).then_inc(small_up, 1)
            act.wait_ge(keys_up, STEPS - KEYS_A + 1)
            for b in range(B):
                last = a.activation(keys_x[:, b, KEYS_A:S + 1], keys[:, KEYS_A:S + 1], ACT.Copy,
                                    scale=lane_sel[:, b:b + 1])
            last.then_inc(keys_a, 1)
            act.wait_ge(xt_ps, 2)
            a.activation(xt_s[:, :], bank(5), ACT.Copy, scale=gam_x[:, 0:1]).then_inc(xt_up, 1)
            for t in range(TT):
                act.wait_ge(xw_ps, t + 1)
                a.activation(xw_s[:, t, :], bank(t), ACT.Copy).then_inc(xw_up, 1)
            for k in range(KS):
                act.wait_ge(ld_sub, k + 1)
                a.activation(disp_e[:, k, :, 0:S], disp_e[:, k, :, 0:S], ACT.Exp).then_inc(ld_exp, 1)
            for t in range(TT):
                act.wait_ge(lc_max, t + 1)
                a.activation(comb_e[:, t, :], bank(t), ACT.Exp, bias=c_nmax[:, t:t + 1],
                             accum_out=c_sum[:, t:t + 1]).then_inc(lc_exp, 1)
            for t in range(TT):
                act.wait_ge(disp_ps, t + 1)
                a.activation(disp_t[:, t, :], bank(4 + t), ACT.Copy).then_inc(disp_up, 1)
            act.wait_ge(d_inv_up, 1)
            for n in range(B * KS):
                b, k = divmod(n, KS)
                act.wait_ge(h_ps, n + 1)
                if n >= NHR:
                    act.wait_ge(hy_used, n - NHR + 1)
                a.activation(h_s[:, n % NHR, :], bank(4 + n % 4), ACT.Gelu,
                             scale=d_inv[:, k, b:b + 1]).then_inc(h_up, 1)
            act.wait_ge(xt_ps, 3)
            a.activation(xt_s[:, :], bank(3), ACT.Copy).then_inc(xt_up, 1)
            act.wait_ge(xt_ps, 4)
            a.activation(xt_s[:, :], bank(5), ACT.Copy).then_inc(xt_up, 1)
            act.wait_ge(gd_up, 1)
            a.activation(gexp[:, :], gdiff[:, :], ACT.Exp).then_inc(ge_up, 1)
            for n in range(E * Q):
                e, q = divmod(n, Q)
                act.wait_ge(eh_ps, n + 1)
                if n == 0:
                    act.wait_ge(pads2, 9)
                if e >= 2 and q == 0:
                    act.wait_ge(eo_ps, e - 1)
                a.activation(tokens(ht_s[:, e % 2, q, :]), bank(n % 3)[:, 0:B * S].rearrange("p (b s) -> p b s", b=B),
                             ACT.Gelu, bias=b1_t[:, n:n + 1]).then_inc(eh_up, 1)

        @block.tensor
        def _(pe):
            T = nc.tensor
            pe.wait_ge(consts, 3)

            def keep_warm(times, free_bank=7):
                for _ in range(times):
                    T.matmul(bank(free_bank)[:, 0:P], ones[:, :], ident[:, :], start=True, stop=True)

            def transpose_tokens(n, to):
                for t in range(TT):
                    if True:
                        pe.wait_ge(xn_up, TT * (n - 1) + t + 1)
                    last = T.transpose(bank(to)[:, t * P:(t + 1) * P], xn_s[:, t, :], ident[:, :])
                last.then_inc(xt_ps, 1)

            def query_norms():
                transpose_tokens(1, 6)
                keep_warm(12)
                pe.wait_ge(xt_up, 2)
                T.matmul(bank(6), ones[:, :], xsq_s[:, :], start=True, stop=True).then_inc(bb_ps, 1)

            def transpose_ctx(k):
                pe.wait_ge(ctx_part[k // GPB], 32)
                if k >= 3:
                    pe.wait_ge(ctx_up, k - 2)
                for i in range(TG):
                    last = T.transpose(bank(k % 3)[:, i * N:(i + 1) * N], ctx_n[0:N, TG * k + i, :],
                                       ident[0:N, 0:N])
                last.then_inc(ctx_ps, 1)

            def products(n):
                b, h = divmod(n, 2)
                c0, c1 = HALVES[h]
                pe.wait_ge(ctx_up, GPB * b + (c1 + TG - 1) // TG)
                if n >= 3:
                    pe.wait_ge(prod_up, n - 2)
                for c in range(c0, c1):
                    last = T.matmul(bank(3 + n % 3)[0:N, (c - c0) * S:(c - c0 + 1) * S], ctx_t[:, C * b + c, :],
                                    xt_s[:, SP * b:SP * b + S], start=True, stop=True)
                last.then_inc(prod_ps, 1)

            def weights_by_feature():
                pe.wait_ge(small_in, SMALL_ALL)
                for h in range(2):
                    T.transpose(bank(7)[:, h * D:(h + 1) * D], wc_n[:, h, :], ident[:, :])
                T.transpose(bank(7)[:, 2 * D:2 * D + E * Q], b1_n[:, :], ident[0:E * Q, 0:E * Q]).then_inc(small_ps, 1)
                pe.wait_ge(se_up, KS)
                pe.wait_ge(prod_up, 2 * B)
                for k in range(KS):
                    last = T.transpose(bank(5)[:, k * P:(k + 1) * P], se_n[:, k, :], ident[:, :])
                last.then_inc(small_ps, 1)

            keep_warm(START_WARM)
            for k in range(GPB):
                transpose_ctx(k)
            query_norms()
            for b in range(1, B):
                transpose_ctx(GPB * b)
                keep_warm(1)
                products(2 * b - 2)
                transpose_ctx(GPB * b + 1)
                keep_warm(1)
                products(2 * b - 1)
                transpose_ctx(GPB * b + 2)
            products(2 * B - 2)
            products(2 * B - 1)
            pe.wait_ge(prod_up, 2 * B)
            pe.wait_ge(pads, 7)
            for n in range(ND):
                if n >= 3:
                    pe.wait_ge(relu_up, n - 2)
                for i in range(DG):
                    last = T.matmul(bank(n % 3)[:, i * N:(i + 1) * N], prod[0:R, DG * n + i, :], turn[0:R, :],
                                    start=True, stop=True)
                last.then_inc(dist_ps, 1)
                if n == SMALL_AT:
                    weights_by_feature()
            pe.wait_ge(relu_up, ND)
            pe.wait_ge(keys_a, 1)
            T.matmul(keys_b[0:N, :, KEYS_A:S + 1], ones[:, 0:N], keys_x[:, :, KEYS_A:S + 1], start=True, stop=True)
            pe.wait_ge(small_up, 3)
            pe.wait_ge(keys_up, STEPS - WARM_AT)
            keep_warm(KEYS_WARM)
            pe.wait_ge(keys_z, 1)
            T.matmul(keys_b[0:N, :, 0:KEYS_A], ones[:, 0:N], keys_x[:, :, 0:KEYS_A],
                     start=True, stop=True).then_inc(kb_ps, 1)
            keep_warm(MASK_WARM)
            pairs = ctx_n[0:N, :, :].rearrange("p (t h c) d -> p t h c d", h=2, c=C)
            for c in range(C):
                pe.wait_ge(mask_up, c + 1)
                for t in range(TT):
                    last = T.matmul(bank(1 + t)[:, 0:2 * D], mask[0:N, c, 2 * t:2 * t + 2, :].rearrange("p h s -> p (h s)"),
                                    pairs[:, t, :, c, :], start=(c == 0), stop=(c == C - 1))
            last.then_inc(exp_ps, 1)

            keep_warm(NORM_WARM)
            transpose_tokens(2, 5)
            pe.wait_ge(xt_up, 3)
            pe.wait_ge(w12_in, 32)
            for t in range(TT):
                T.matmul(bank(t), xt_s[:, t * P:(t + 1) * P], w1_s[:, :], start=True, stop=True).then_inc(xw_ps, 1)
            pe.wait_ge(small_up, 3)
            for k in range(KS):
                T.matmul(bank(4 + k)[:, 0:B * S], se_t[:, k * P:(k + 1) * P], tokens(xt_s[:, :]),
                         start=True, stop=True).then_inc(ld_ps, 1)
            for t in range(TT):
                pe.wait_ge(xw_up, t + 1)
                T.matmul(bank(t), xt_s[:, t * P:(t + 1) * P], se_t[:, :], start=True, stop=True).then_inc(lc_ps, 1)
            pe.wait_ge(ld_exp, KS)
            pe.wait_ge(pads2, 7)
            for t in range(TT):
                for k in range(KS):
                    last = T.transpose(bank(4 + t)[:, k * P:(k + 1) * P],
                                       disp_e[:, k, 2 * t:2 * t + 2, :].rearrange("p h s -> p (h s)"), ident[:, :])
                last.then_inc(disp_ps, 1)
            pe.wait_ge(lc_exp, TT)
            for k in range(KS):
                for t in range(TT):
                    last = T.transpose(bank(k)[:, t * P:(t + 1) * P], comb_e[:, t, k * P:(k + 1) * P], ident[:, :])
                last.then_inc(comb_ps, 1)

            def hidden(n):
                b, k = divmod(n, KS)
                t, h = divmod(b, 2)
                if k == 0 and h == 0:
                    pe.wait_ge(disp_up, TT if n == 0 else t + 1)
                if n >= 4:
                    pe.wait_ge(h_up, n - 3)
                T.matmul(bank(4 + n % 4), disp_t[SP * h:SP * h + S, t, k * P:(k + 1) * P],
                         xw_s[SP * h:SP * h + S, t, :], start=True, stop=True).then_inc(h_ps, 1)

            def combined(n):
                b, k = divmod(n, KS)
                pe.wait_ge(h_up, n + 1)
                if k == 0:
                    pe.wait_ge(comb_up, KS)
                    if b >= 2:
                        pe.wait_ge(y_up, b - 1)
                for q in range(Q):
                    last = T.matmul(bank(b % 2)[:, q * S:(q + 1) * S], h_s[:, n % NHR, q * P:(q + 1) * P],
                                    comb_t[:, k, SP * b:SP * b + S], start=(k == 0 and q == 0), stop=(k == KS - 1),
                                    skip_group_check=True)
                last.then_inc(hy_used, 1)

            pe.wait_ge(xw_up, TT)
            AHEAD = 3
            for n in range(B * KS + AHEAD):
                if n < B * KS:
                    hidden(n)
                if n >= AHEAD:
                    combined(n - AHEAD)
            pe.wait_ge(y_up, B)
            pe.wait_ge(pads2, 8)
            for t in range(TT):
                for q in range(Q):
                    last = T.matmul(bank(2)[:, t * D:(t + 1) * D], y_t[:, q, t * P:(t + 1) * P], w2_s[:, q, :],
                                    start=(q == 0), stop=(q == Q - 1))
                last.then_inc(f0_ps, 1)

            keep_warm(NORM_WARM)
            transpose_tokens(3, 3)
            pe.wait_ge(small_up, 2)
            pe.wait_ge(csum_up, 1)
            for t in range(TT):
                dst = bank(4)[:, t * D:(t + 1) * D]
                T.matmul(dst, csum_b[:, 2 * t:2 * t + 2, :].rearrange("p h s -> p (h s)"), wc_t[:, 1, :],
                         start=True, stop=False)
                T.matmul(dst, ones[0:1, :], bc_s[0:1, :], start=False, stop=False)
                if t == 0:
                    pe.wait_ge(xt_up, 4)
                T.matmul(dst, xt_s[:, t * P:(t + 1) * P], wc_t[:, 0, :], start=False, stop=True).then_inc(xa_ps, 1)

            keep_warm(NORM_WARM)
            transpose_tokens(4, 5)
            pe.wait_ge(xt_up, 5)
            for t in range(TT):
                dst = bank(6)[:, t * E:(t + 1) * E]
                T.matmul(dst, xt_s[:, t * P:(t + 1) * P], gw_s[:, :], start=True, stop=False)
                last = T.matmul(dst, ones[0:1, :], gb_s[0:1, :], start=False, stop=True)
            last.then_inc(g_ps, 1)

            def expert_hidden(e):
                if e == 0:
                    pe.wait_ge(ew1_in, 16)
                for q in range(Q):
                    n = e * Q + q
                    if n >= 3:
                        pe.wait_ge(eh_up, n - 2)
                    T.matmul(bank(n % 3)[:, 0:B * S], ew1_s[:, e, q * P:(q + 1) * P], tokens(xt_s[:, :]),
                             start=True, stop=True).then_inc(eh_ps, 1)

            def expert_out(e):
                if e == 0:
                    pe.wait_ge(ew2_in, 16)
                if e >= 2:
                    pe.wait_ge(eo_up, TT * (e - 1))
                pe.wait_ge(eh_up, Q * (e + 1))
                for t in range(TT):
                    for q in range(Q):
                        last = T.matmul(bank(4 + e % 2)[:, t * D:(t + 1) * D], ht_s[:, e % 2, q, t * P:(t + 1) * P],
                                        ew2_s[:, e, q, :], start=(q == 0), stop=(q == Q - 1))
                last.then_inc(eo_ps, 1)

            def second_biases():
                pe.wait_ge(wt_up, 1)
                for t in range(TT):
                    last = T.transpose(bank(7)[0:E, t * P:(t + 1) * P], wt[:, t, :], ident[:, :])
                last.then_inc(wtt_ps, 1)
                pe.wait_ge(wtt_up, 1)
                for t in range(TT):
                    last = T.matmul(bank(3)[:, t * D:(t + 1) * D], wt_t[:, t * P:(t + 1) * P], b2_s[:, :],
                                    start=True, stop=True)
                last.then_inc(b2_ps, 1)

            expert_hidden(0)
            for e in range(E):
                if e + 1 < E:
                    expert_hidden(e + 1)
                if e == 0:
                    second_biases()
                expert_out(e)

        @block.vector
        def _(dve):
            v = nc.vector
            done = [0]

            def link(ins):
                done[0] += 1
                ins.then_inc(dve_c, 1)
                dve.wait_ge(dve_c, done[0])

            def mark(ins):
                done[0] += 1
                ins.then_inc(dve_c, 1)

            def row_stats():
                for t in range(TT):
                    mark(v.bn_stats(stats[:, t, :], x_s[:, t, :]))
                dve.wait_ge(dve_c, done[0])
                for t in range(TT):
                    mark(v.bn_aggr(mv[:, t, :], stats[:, t, :]))
                dve.wait_ge(dve_c, done[0])

            def layer_norm(n):
                row_stats()
                v.tensor_scalar(vv[:, 1, :], mv[:, :, 1], LN_EPS, None, ALU.add).then_inc(var_up, 1)
                dve.wait_ge(pool_pow, n)
                for t in range(TT):
                    v.tensor_scalar(xn_s[:, t, :], x_s[:, t, :], mv[:, t, 0:1], vr[:, 0, t:t + 1],
                                    ALU.subtract, ALU.mult).then_inc(xn_up, 1)

            v.memset(x_s[:, :, :], 0.0).then_inc(zeroed, 1)
            dve.wait_ge(consts, CONSTS)
            link(v.tensor_scalar(lane_m[:, :], lane_i[:, :], LPB - 1, None, ALU.bitwise_and))
            link(v.tensor_copy(lane_f[:, :], lane_m[:, :]))
            link(v.tensor_scalar(lane4[:, :], lane_f[:, :], 4.0 * N, None, ALU.mult))
            mark(v.memset(cost[:, 0, :], INF))
            link(v.tensor_scalar(key4[:, :], key_row[:, :], lane4[:, 0:1], None, ALU.add))
            assert done[0] == 5
            link(v.tensor_scalar(lane0[:, :], lane_f[:, :], 1.0, -INF, ALU.is_equal, ALU.mult))
            link(v.tensor_scalar(cost[:, 0, 0:1], lane0[:, :], INF, None, ALU.add))
            v.tensor_scalar(keys[:, STEPS:STEPS + 1], lane_f[:, :], 0.0, float(LAST_KEY),
                            ALU.is_gt, ALU.mult).then_inc(keys_up, 1)

            dve.wait_ge(x_in, 32)
            layer_norm(1)

            dve.wait_ge(se_in, 16)
            for k in range(KS):
                if k >= 2:
                    dve.wait_ge(dve_c, done[0] - 1)
                mark(v.tensor_tensor_reduce(junk_v[:, k % 2, :], se_n[:, k, :], se_n[:, k, :], 1.0, 0.0,
                                            ALU.mult, ALU.add, se_sq[:, k:k + 1]))
            dve.wait_ge(dve_c, done[0])
            v.tensor_scalar(se_r[:, :], se_sq[:, :], 1.0 / D, None, ALU.mult).then_inc(se_sum, 1)
            dve.wait_ge(se_root, 1)
            link(v.tensor_scalar(se_r[:, :], se_r[:, :], RMS_EPS / D ** 0.5, None, ALU.max))
            link(v.reciprocal(se_r[:, :], se_r[:, :]))
            for k in range(KS):
                v.tensor_scalar(se_n[:, k, :], se_n[:, k, :], se_r[:, k:k + 1], None, ALU.mult).then_inc(se_up, 1)

            nsq = [0]

            def square_sums(b):
                dve.wait_ge(ctx_part[b], 32)
                for c in range(ACT_SQ + POOL_SQ, C):
                    if nsq[0] >= 2:
                        dve.wait_ge(aa_up, nsq[0] - 1)
                    v.tensor_tensor_reduce(junk_v[0:N, nsq[0] % 2, :], ctx_n[0:N, C * b + c, :],
                                           ctx_n[0:N, C * b + c, :], 1.0, 0.0, ALU.mult, ALU.add,
                                           aa_n[0:N, lane(b, c):lane(b, c) + 1]).then_inc(aa_up, 1)
                    nsq[0] += 1

            def store_products(b):
                dve.wait_ge(bb_rows, b + 1)
                dve.wait_ge(aa_act, ACT_SQ * (b + 1))
                dve.wait_ge(aa_up, (C - ACT_SQ - POOL_SQ) * (b + 1))
                dve.wait_ge(aa_pool, b + 1)
                for h, (c0, c1) in enumerate(HALVES):
                    n = 2 * b + h
                    dve.wait_ge(prod_ps, n + 1)
                    v.tensor_tensor(diagonal(b, c0, c1, 0, N),
                                    bank(3 + n % 3)[0:N, 0:(c1 - c0) * S].rearrange("p (c s) -> p c s", s=S),
                                    aa_n[0:N, lane(b, c0):lane(b, c1), None].to_broadcast([N, c1 - c0, S]),
                                    ALU.add).then_inc(prod_up, 1)

            def add_squares(b):
                dve.wait_ge(sq_up, b + 1)
                v.tensor_reduce(aa_n[0:N, lane(b, ACT_SQ):lane(b, ACT_SQ + POOL_SQ)], squares[0:N, b % 2, :, :],
                                AX.X, ALU.add).then_inc(aa_pool, 1)

            def norm_rows(b):
                if b == 0:
                    dve.wait_ge(bb_up, 1)
                    dve.wait_ge(pads, 5)
                v.tensor_copy(diagonal(b, 0, C, QUARTER, R),
                              bb_s[QUARTER:R, b:b + 1, 0:S].to_broadcast([R - QUARTER, C, S])).then_inc(bb_rows, 1)

            square_sums(0)
            norm_rows(0)
            for b in range(1, B):
                square_sums(b)
                add_squares(b - 1)
                norm_rows(b)
                store_products(b - 1)
            add_squares(B - 1)
            store_products(B - 1)

            from_above = [i if i % LPB == 0 else i - 1 for i in range(32)]

            def flag_left(s, h):
                v.tensor_tensor(left_f[:, s, N // 2 * h:N // 2 * (h + 1)], cost[:, s, 1 + N // 2 * h:1 + N // 2 * (h + 1)],
                                cost[:, s + 1, N // 2 * h:N // 2 * (h + 1)], ALU.is_lt).then_inc(flags_up, 1)

            for s in range(STEPS):
                if s >= 1:
                    dve.wait_ge(wave_r, s)
                v.stream_shuffle(cost[:, s + 1, 0:1], cost[:, s, N:R], from_above)
                v.tensor_tensor(m_s[:, s % 2, :], cost[:, s, 1:R], cost[:, s, 0:N], ALU.min).then_inc(wave_m, 1)
                if s >= 1:
                    flag_left(s - 1, 0)
                if s % DG == 0:
                    dve.wait_ge(dist_up, s // DG + 1)
                dve.wait_ge(wave_m, s + 1)
                v.tensor_tensor_scan(cost[:, s + 1, 1:R], m_s[:, s % 2, :], cost[:, s + 1, 1:R],
                                     cost[:, s + 1, 0:1], ALU.min, ALU.add).then_inc(wave_r, 1)
                if s >= 1:
                    flag_left(s - 1, 1)
            dve.wait_ge(wave_r, STEPS)
            flag_left(STEPS - 1, 0)
            flag_left(STEPS - 1, 1)
            v.memset(below[:, :, 0:1], 1.0)
            dve.wait_ge(flags_up, 2 * STEPS)

            from_below = [i if i % LPB == 0 else (i + 1) % 32 for i in range(32)]

            def merge_flags(s0, s1):
                rows = left_f[:, s0:s1, :]
                v.tensor_tensor(rows, rows, diag_f[:, s0:s1, :], ALU.max).then_inc(merge_up, 1)

            for n in range(NSP - 1, NSP - 1 - NMERGE, -1):
                dve.wait_ge(flags_d, n + 1 if n == NSP - 2 else NSP)
                merge_flags(*SPANS[n])
            s0, s1 = SPANS[-1]
            rows = key_t[:, s0:s1, 1:R]
            dve.wait_ge(key_up, NSP)
            link(v.tensor_tensor(rows, rows, key4[:, None, :].to_broadcast([P, s1 - s0, N]), ALU.mult))
            dve.wait_ge(merge_up, 1)
            link(v.tensor_tensor(rows, rows, left_f[:, s0:s1, :], ALU.mult))
            for s in range(STEPS - 1, -1, -1):
                i = STEPS - 1 - s
                dve.wait_ge(keys_up, i + 1)
                v.stream_shuffle(key_t[:, s, 0:1], keys[:, s + 1:s + 2], from_below)
                v.tensor_scalar(below[:, i % 2, 1:R], key4[:, :], keys[:, s + 1:s + 2], None,
                                ALU.is_lt).then_inc(below_up, 1)
                if i < AHEAD_S:
                    merge_flags(AHEAD_S - 1 - i, AHEAD_S - i)
                for n in range(NSP - 1):
                    if s == SPANS[n][1] - 1:
                        dve.wait_ge(picked_up, NSP - 1 - n)
                dve.wait_ge(below_up, i + 1)
                v.tensor_tensor_reduce(hit[:, i % 2, :], below[:, i % 2, :], key_t[:, s, :], 1.0, 0.0,
                                       ALU.mult, ALU.max, keys[:, s:s + 1]).then_inc(keys_up, 1)

            dve.wait_ge(keys_up, STEPS + 1)
            v.tensor_tensor(keys_x[:, :, 0:KEYS_A], keys[:, None, 0:KEYS_A].to_broadcast([P, B, KEYS_A]),
                            lane_sel[:, :, None].to_broadcast([P, B, KEYS_A]), ALU.mult).then_inc(keys_z, 1)
            dve.wait_ge(pads2, 6)
            dve.wait_ge(kb_ps, 1)
            for c in range(C):
                if c >= 2:
                    dve.wait_ge(mask_up, c - 1)
                v.tensor_scalar(under[0:N, c % 2, :, :], keys_b[0:N, :, 1:S + 1], row4[0:N, c:c + 1], None,
                                ALU.is_gt).then_inc(under_up, 1)
                if c >= 1:
                    dve.wait_ge(under_up, c)
                    v.scalar_tensor_tensor(mask[0:N, c - 1, :, 0:S], keys_b[0:N, :, 0:S], row4b[0:N, c - 1:c],
                                           under[0:N, (c - 1) % 2, :, :], ALU.is_lt, ALU.mult).then_inc(mask_up, 1)
            dve.wait_ge(under_up, C)
            v.scalar_tensor_tensor(mask[0:N, C - 1, :, 0:S], keys_b[0:N, :, 0:S], row4b[0:N, C - 1:C],
                                   under[0:N, (C - 1) % 2, :, :], ALU.is_lt, ALU.mult).then_inc(mask_up, 1)
            link(v.tensor_reduce(csum[:, :], csum_g[:, :, :], AX.X, ALU.add))
            link(v.tensor_scalar(csum[:, :], csum[:, :], 1.0 / L, None, ALU.mult))
            v.tensor_copy(csum_b[:, :, :], csum[:, :, None].to_broadcast([P, B, SP])).then_inc(csum_up, 1)
            link(v.tensor_copy(rtemp[:, :], temp_s[:, :]))
            link(v.reciprocal(rtemp[:, :], rtemp[:, :]))

            dve.wait_ge(exp_ps, 1)
            dve.wait_ge(tg_up, 2)
            for h in range(2):
                rows = slice(SP * h, SP * h + SP)
                mark(v.scalar_tensor_tensor(x_s[rows, :, :], ps[rows, 1:1 + TT, h * D:(h + 1) * D], tgx[rows, 0:1],
                                            x_s[rows, :, :], ALU.mult, ALU.add))
            dve.wait_ge(dve_c, done[0])
            row_stats()
            mark(v.tensor_copy(vv[:, 0, :], mv[:, :, 1]))
            v.tensor_scalar(vv[:, 1, :], mv[:, :, 1], LN_EPS, None, ALU.add).then_inc(var_up, 1)
            dve.wait_ge(pool_pow, 2)
            link(v.scalar_tensor_tensor(den[:, :], vr[:, 1, :], RMS_EPS / D ** 0.5, vr[:, 0, :], ALU.mult, ALU.max))
            link(v.reciprocal(fac[:, :], den[:, :]))
            for t in range(TT):
                v.tensor_scalar(xn_s[:, t, :], x_s[:, t, :], mv[:, t, 0:1], fac[:, t:t + 1],
                                ALU.subtract, ALU.mult).then_inc(xn_up, 1)
            for k in range(KS):
                dve.wait_ge(ld_ps, k + 1)
                logits = bank(4 + k)[:, 0:B * S].rearrange("p (b s) -> p b s", b=B)
                link(v.reduce_max(d_max[:, k, :], logits, AX.X))
                v.tensor_tensor(disp_e[:, k, :, 0:S], logits, d_max[:, k, :, None].to_broadcast([P, B, S]),
                                ALU.subtract).then_inc(ld_sub, 1)
            for t in range(TT):
                dve.wait_ge(lc_ps, t + 1)
                v.tensor_reduce(c_nmax[:, t:t + 1], bank(t), AX.X, ALU.max, negate=True).then_inc(lc_max, 1)
            for k in range(KS):
                dve.wait_ge(ld_exp, k + 1)
                mark(v.tensor_reduce(d_sum[:, k, :], disp_e[:, k, :, 0:S], AX.X, ALU.add))
            dve.wait_ge(dve_c, done[0])
            v.reciprocal(d_inv[:, :, :], d_sum[:, :, :]).then_inc(d_inv_up, 1)
            for k in range(KS):
                dve.wait_ge(comb_ps, k + 1)
                v.tensor_copy(comb_t[:, k, :], bank(k)).then_inc(comb_up, 1)
            dve.wait_ge(lc_exp, TT)
            link(v.reciprocal(c_inv[:, :], c_sum[:, :]))
            link(v.tensor_scalar(tgr[:, :], c_inv[:, :], tgf[:, 0:1], None, ALU.mult))
            for b in range(B):
                dve.wait_ge(hy_used, KS * (b + 1))
                v.tensor_copy(y_t[:, :, SP * b:SP * b + S],
                              bank(b % 2)[:, 0:Q * S].rearrange("p (q s) -> p q s", q=Q)).then_inc(y_up, 1)
            for t in range(TT):
                dve.wait_ge(f0_ps, TT)
                mark(v.scalar_tensor_tensor(x_s[:, t, :], bank(2)[:, t * D:(t + 1) * D], tgr[:, t:t + 1], x_s[:, t, :],
                                            ALU.mult, ALU.add))
            dve.wait_ge(dve_c, done[0])
            layer_norm(3)
            for t in range(TT):
                dve.wait_ge(xa_ps, TT)
                mark(v.scalar_tensor_tensor(x_s[:, t, :], bank(4)[:, t * D:(t + 1) * D], tgx[:, 1:2], x_s[:, t, :],
                                            ALU.mult, ALU.add))
            dve.wait_ge(dve_c, done[0])
            layer_norm(4)
            dve.wait_ge(g_ps, 1)
            link(v.tensor_scalar(gates[:, :, :].rearrange("p t e -> p (t e)"), bank(6)[:, 0:TT * E], rtemp[:, 0:1],
                                 None, ALU.mult))
            for t in range(TT):
                mark(v.max(top[:, t, :], gates[:, t, :]))
            dve.wait_ge(dve_c, done[0])
            v.tensor_tensor(gdiff[:, :], top[:, :, 1], top[:, :, 0], ALU.subtract).then_inc(gd_up, 1)
            for t in range(TT):
                mark(v.max_index(top_i[:, t, :], top[:, t, :], gates[:, t, :]))
            dve.wait_ge(dve_c, done[0])
            mark(v.tensor_copy(top_f[:, :, :], top_i[:, :, 0:2]))
            dve.wait_ge(ge_up, 1)
            link(v.tensor_scalar(gden[:, :], gexp[:, :], 1.0, None, ALU.add))
            link(v.reciprocal(wgt[:, 0, :], gden[:, :]))
            link(v.tensor_tensor(wgt[:, 1, :], wgt[:, 0, :], gexp[:, :], ALU.mult))
            for t in range(TT):
                for j, dst in ((0, wt1), (1, wt2)):
                    mark(v.tensor_scalar(dst[:, t, :], e_iota[:, :], top_f[:, t, j:j + 1], wgt[:, j, t:t + 1],
                                         ALU.is_equal, ALU.mult))
            dve.wait_ge(dve_c, done[0])
            v.tensor_tensor(wt[:, :, :], wt1[:, :, :], wt2[:, :, :], ALU.add).then_inc(wt_up, 1)
            dve.wait_ge(wtt_ps, 1)
            v.tensor_copy(wt_t[:, :], bank(7)[0:E, :]).then_inc(wtt_up, 1)
            dve.wait_ge(b2_ps, 1)
            v.tensor_copy(acc[:, :, :].rearrange("p t d -> p (t d)"), bank(3)).then_inc(acc_up, 1)
            for e in range(E):
                dve.wait_ge(eo_ps, e + 1)
                for t in range(TT):
                    dve.wait_ge(acc_up, 1) if e == 0 else dve.wait_ge(eo_up, TT * (e - 1) + t + 1)
                    v.scalar_tensor_tensor(acc[:, t, :], bank(4 + e % 2)[:, t * D:(t + 1) * D], wt[:, t, e:e + 1],
                                           acc[:, t, :], ALU.mult, ALU.add).then_inc(eo_up, 1)
            for t in range(TT):
                dve.wait_ge(eo_up, TT * (E - 1) + t + 1)
                v.scalar_tensor_tensor(x_s[:, t, :], acc[:, t, :], tgf[:, 1:2], x_s[:, t, :],
                                       ALU.mult, ALU.add).then_inc(fin_up, 1)


_INS = ['x', 'ctx_1024', 'g_xattn', 'g_ffn', 'L0_ffn_gamma_x', 'L0_ffn_gamma_slot', 'L0_ffn_slot_embeds',
        'L0_ffn_w1', 'L0_ffn_w2', 'L1_xattn_W', 'L1_xattn_b', 'L1_ffn_W1', 'L1_ffn_b1', 'L1_ffn_W2', 'L1_ffn_b2',
        'L1_ffn_gate_w', 'L1_ffn_gate_b', 'L1_ffn_temperature']


def kernel(**inputs):
    import numpy as _np
    import concourse.bacc as _bacc
    from concourse import mybir as _mybir
    from concourse.bass_utils import run_bass_kernel_spmd as _run

    nc = _bacc.Bacc("TRN2", target_bir_lowering=False, num_devices=1)
    arrays, args = {}, []
    for name in _INS:
        a = _np.ascontiguousarray(inputs[name])
        if a.ndim == 0:
            a = a.reshape(1)
        arrays[f"in_{name}_dram"] = a
        args.append(nc.dram_tensor(f"in_{name}_dram", a.shape, _mybir.dt.from_np(a.dtype), kind="ExternalInput").ap())
    shape = inputs['x'].shape
    out = nc.dram_tensor("out_0_dram", tuple(shape), _mybir.dt.float32, kind="ExternalOutput").ap()
    gated_stack(nc, *args, out)
    r = _run(nc, [arrays], core_ids=[0])
    return r.results[0]["out_0_dram"]
```

```python
from contextlib import ExitStack

import concourse.bass as bass
from concourse import mybir

F32 = mybir.dt.float32
BF16 = mybir.dt.bfloat16
I32 = mybir.dt.int32
ALU = mybir.AluOpType
ACT = mybir.ActivationFunctionType
AX = mybir.AxisListType

P = 128
LN_EPS = 1e-5
RMS_EPS = 1e-12
TINY = 1e-37
INF = 1e30
PAD_D2 = 1e35


def gated_stack(nc, x, ctx_in, g_xattn, g_ffn, gamma_x, gamma_slot, slot_embeds, w1, w2, Wc, bc,
                eW1, eb1, eW2, eb2, gate_w, gate_b, temperature, out):
    B, S, D = x.shape
    L = ctx_in.shape[1]
    LPB = P // B
    C = LPB - 1
    N = L // C
    R = N + 1
    STEPS = S + C - 1
    TT = B // 2
    SP = P // 2
    NS, NT, _ = slot_embeds.shape
    SLOTS = NS * NT
    KS = SLOTS // P
    HID = w1.shape[1]
    Q = HID // P
    E = eW1.shape[0]
    assert D == P and C * N == L and B * LPB == P and S <= SP
    LAST_KEY = 4 * L + 8
    TG = 5
    GPB = C // TG
    NG = B * GPB
    HALVES = ((0, 8), (8, C))
    DG = 5
    DSPANS = [(0, 1), (1, DG)] + [(n, n + DG) for n in range(DG, STEPS, DG)]
    ND = len(DSPANS)
    SPANS = [(DG * n, DG * n + DG) for n in range(STEPS // DG - 1)] + [(STEPS - DG, STEPS - 2), (STEPS - 2, STEPS)]
    NSP = len(SPANS)
    NMERGE = 3
    AHEAD_S = SPANS[NSP - NMERGE][0]
    SMALL_AT = 2
    SIDE = 2.0 ** -12
    assert 4 * L * SIDE < 2
    KEYS_A = 14
    WARM_AT = 8
    KEYS_WARM, MASK_WARM, NORM_WARM = 20, 7, (1, 1, 6)
    TAIL_C = 4
    XT_BANKS = {2: (5, 6, 7, 0), 3: (0, 1, 2, 3), 4: (0, 1, 2, 3)}
    H_BANKS = (5, 6, 7, 4)
    LAST_BANKS = (3, 6, 7, 5)
    START_WARM = 10
    ACT_SQ = 5
    POOL_SQ = 8

    with ExitStack() as stack:
        def sb(name, shape, dt=F32):
            return stack.enter_context(nc.sbuf_tensor(name, shape, dt))

        def sem(name):
            return stack.enter_context(nc.semaphore(name))

        ctx_n = sb("ctx_n", [P, B * C, D])
        region_x = sb("region_x", [P, B * L])
        ctx_t = region_x[:, :].rearrange("p (g n) -> p g n", n=N)
        key_t = region_x[:, 0:STEPS * R].rearrange("p (s n) -> p s n", n=R)
        ew1_s = region_x[:, 7072:7072 + E * HID].rearrange("p (e f) -> p e f", e=E)
        disp_e = region_x[:, 0:KS * B * SP].rearrange("p (k b s) -> p k b s", k=KS, b=B)
        comb_e = region_x[:, 2048:2048 + TT * SLOTS].rearrange("p (t n) -> p t n", t=TT)
        xw_s = region_x[:, 4096:4096 + TT * HID].rearrange("p (t f) -> p t f", t=TT)
        ht_s = region_x[:, 0:2 * Q * B * SP].rearrange("p (r q n) -> p r q n", r=2, q=Q)
        region_d = sb("region_d", [P, STEPS * P])
        prod = region_d[:, :].rearrange("p (s l) -> p s l", l=P)
        flags = region_d[:, :].bitcast(BF16).rearrange("p (s n) -> p s n", n=2 * P)
        left_f = flags[:, :, 0:N]
        diag_f = flags[:, :, N:2 * N]
        mask = region_d[:, 0:C * B * SP].rearrange("p (c b s) -> p c b s", c=C, b=B)
        under = region_d[:, 7680:7680 + 2 * B * S].rearrange("p (r b s) -> p r b s", r=2, b=B)
        acc = region_d[:, 0:TT * D].rearrange("p (t d) -> p t d", t=TT)
        wt_t = region_d[0:E, 512:512 + TT * P]
        disp_t = region_d[:, 0:TT * SLOTS].rearrange("p (t n) -> p t n", t=TT)
        comb_t = region_d[:, 2048:2048 + KS * B * SP].rearrange("p (k n) -> p k n", k=KS)
        NHR = 4
        h_s = region_d[:, 4096:4096 + NHR * HID].rearrange("p (r f) -> p r f", r=NHR)
        y_t = region_d[:, 6144:6144 + Q * B * SP].rearrange("p (q n) -> p q n", q=Q)
        region_w = sb("region_w", [P, (STEPS + 1) * R])
        cost = region_w[:, :].rearrange("p (s r) -> p s r", r=R)
        squares = region_w[:, 1024:1024 + 2 * POOL_SQ * D].rearrange("p (r c d) -> p r c d", r=2, d=D)
        ew2_s = region_w[:, 0:E * HID].rearrange("p (e q d) -> p e q d", e=E, q=Q)

        x_s = sb("x_s", [P, TT, D])
        xn_s = sb("xn_s", [P, TT, D])
        xt_s = sb("xt_s", [P, B * SP])
        xsq_s = sb("xsq_s", [P, B * SP])
        hit = xsq_s[:, 0:2 * R].rearrange("p (r n) -> p r n", n=R)
        below = xsq_s[:, 2 * R:4 * R].rearrange("p (r n) -> p r n", n=R)
        bb_s = sb("bb_s", [P, B, SP])
        stats = sb("stats", [P, TT, 6])
        mv = sb("mv", [P, TT, 2])
        eps = sb("eps", [P, 1])
        vr = sb("vr", [P, 2, TT])
        den = sb("den", [P, TT])
        fac = sb("fac", [P, TT])
        ident = sb("ident", [P, P])
        ones = sb("ones", [P, P])
        aa_n = sb("aa_n", [P, P])
        turn = sb("turn", [P, N])
        junk_v = sb("junk_v", [P, 2, D])
        junk_a = sb("junk_a", [P, 2, D])
        lane_i = sb("lane_i", [P, 1], I32)
        lane_m = sb("lane_m", [P, 1], I32)
        lane_f = sb("lane_f", [P, 1])
        lane4 = sb("lane4", [P, 1])
        tiny = sb("tiny", [P, 1])
        lane0 = sb("lane0", [P, 1])
        key_row = sb("key_row", [P, N])
        key4 = sb("key4", [P, N])
        m_s = sb("m_s", [P, 2, N])
        keys = sb("keys", [P, STEPS + 1])
        lane_sel = sb("lane_sel", [P, B])
        keys_x = sb("keys_x", [P, B, S + 1])
        row4 = sb("row4", [P, C])
        row4b = sb("row4b", [P, C])
        csum_g = sb("csum_g", [P, B, GPB])
        csum = sb("csum", [P, B])
        csum_b = sb("csum_b", [P, B, SP])
        gx_b = sb("gx_b", [P, 2])
        gf_b = sb("gf_b", [P, 2])
        tgx = sb("tgx", [P, 2])
        tgf = sb("tgf", [P, 2])
        tgr = sb("tgr", [P, TT])
        gam_x = sb("gam_x", [P, 1])
        gam_s = sb("gam_s", [P, 1])
        se_n = sb("se_n", [P, KS, D])
        se_sq = sb("se_sq", [P, KS])
        se_r = sb("se_r", [P, KS])
        se_t = sb("se_t", [P, SLOTS])
        w1_s = sb("w1_s", [P, HID])
        w2_s = sb("w2_s", [P, Q, D])
        wc_n = sb("wc_n", [P, 2, D])
        wc_t = sb("wc_t", [P, 2, D])
        bc_s = sb("bc_s", [1, D])
        b1_n = sb("b1_n", [E * Q, P])
        b1_t = sb("b1_t", [P, E * Q])
        b2_s = sb("b2_s", [E, D])
        gw_s = sb("gw_s", [P, E])
        gb_b = sb("gb_b", [P, E])
        temp_s = sb("temp_s", [P, 1])
        rtemp = sb("rtemp", [P, 1])
        d_max = sb("d_max", [P, KS, B])
        d_sum = sb("d_sum", [P, KS, B])
        d_inv = sb("d_inv", [P, KS, B])
        c_nmax = sb("c_nmax", [P, TT])
        c_sum = sb("c_sum", [P, TT])
        c_inv = sb("c_inv", [P, TT])
        gates = sb("gates", [P, TT, E])
        top = sb("top", [P, TT, 8])
        top_i = sb("top_i", [P, TT, 8], mybir.dt.uint32)
        top_f = sb("top_f", [P, TT, 2])
        e_iota = sb("e_iota", [P, E])
        gdiff = sb("gdiff", [P, TT])
        gexp = sb("gexp", [P, TT])
        gden = sb("gden", [P, TT])
        wgt = sb("wgt", [P, 2, TT])
        wt1 = sb("wt1", [P, TT, E])
        wt2 = sb("wt2", [P, TT, E])
        wt = sb("wt", [P, TT, E])
        wt_g = sb("wt_g", [P, TT, 2])

        ps = stack.enter_context(nc.psum_tensor("ps", [P, 8, 512], F32))

        x_in = sem("x_in")
        small_in = sem("small_in")
        ctx_part = [[sem(f"ctx_in0_{j}") for j in range(GPB)]] + [[sem(f"ctx_in{b}")] for b in range(1, B)]
        ew1_in = sem("ew1_in")
        ew2_in = sem("ew2_in")
        out_done = sem("out_done")
        zeroed = sem("zeroed")
        consts = sem("consts")
        pads = sem("pads")
        var_up = sem("var_up")
        root_up = sem("root_up")
        dve_c = sem("dve_c")
        xn_up = sem("xn_up")
        xt_ps = sem("xt_ps")
        xt_up = sem("xt_up")
        bb_ps = sem("bb_ps")
        bb_up = sem("bb_up")
        small_ps = sem("small_ps")
        small_up = sem("small_up")
        se_up = sem("se_up")
        ctx_ps = sem("ctx_ps")
        ctx_up = sem("ctx_up")
        prod_ps = sem("prod_ps")
        prod_up = sem("prod_up")
        aa_up = sem("aa_up")
        bb_rows = sem("bb_rows")
        dist_ps = sem("dist_ps")
        dist_up = sem("dist_up")
        wave_m = sem("wave_m")
        wave_r = sem("wave_r")
        flags_up = sem("flags_up")
        gap_up = sem("gap_up")
        sign_up = sem("sign_up")
        key_up = sem("key_up")
        scaled_up = sem("scaled_up")
        picked_up = sem("picked_up")
        below_up = sem("below_up")
        keys_up = sem("keys_up")
        keys_a = sem("keys_a")
        keys_z = sem("keys_z")
        kb_ps = sem("kb_ps")
        mask_up = sem("mask_up")
        exp_ps = sem("exp_ps")
        csum_up = sem("csum_up")
        tg_up = sem("tg_up")
        xw_ps = sem("xw_ps")
        xw_up = sem("xw_up")
        ld_ps = sem("ld_ps")
        ld_sub = sem("ld_sub")
        ld_exp = sem("ld_exp")
        lc_ps = sem("lc_ps")
        lc_max = sem("lc_max")
        lc_exp = sem("lc_exp")
        d_inv_up = sem("d_inv_up")
        disp_ps = sem("disp_ps")
        disp_up = sem("disp_up")
        comb_ps = sem("comb_ps")
        comb_up = sem("comb_up")
        h_ps = sem("h_ps")
        h_up = sem("h_up")
        y_up = sem("y_up")
        hy_used = sem("hy_used")
        f0_ps = sem("f0_ps")
        f0_used = sem("f0_used")
        xa_ps = sem("xa_ps")
        g_ps = sem("g_ps")
        gd_up = sem("gd_up")
        ge_up = sem("ge_up")
        wt_up = sem("wt_up")
        wtt_ps = sem("wtt_ps")
        wtt_up = sem("wtt_up")
        b2_ps = sem("b2_ps")
        eh_ps = sem("eh_ps")
        eh_up = sem("eh_up")
        eo_ps = sem("eo_ps")
        eo_up = sem("eo_up")
        fin_up = sem("fin_up")
        pads2 = sem("pads2")
        aa_pool = sem("aa_pool")
        sq_up = sem("sq_up")
        aa_act = sem("aa_act")
        gap2_up = sem("gap2_up")
        last_flags = sem("last_flags")
        flags_d = sem("flags_d")
        merge_up = sem("merge_up")
        under_up = sem("under_up")
        acc_up = sem("acc_up")
        se_sum = sem("se_sum")
        se_root = sem("se_root")
        g_in = sem("g_in")
        se_in = sem("se_in")
        w12_in = sem("w12_in")
        relu_up = sem("relu_up")

        def bank(i):
            return ps[:, i, :]

        keys_b = bank(0)[:, 0:B * (S + 1)].rearrange("p (b s) -> p b s", b=B)

        def tokens(ap):
            return ap.rearrange("p (b s) -> p b s", b=B)[:, :, 0:S]

        def lane(b, c):
            return LPB * b + 1 + c

        QUARTER = N // 32 * 32

        def diagonal(b, c0, c1, row0, row1):
            base = prod[row0:row1, c0, lane(b, c0):lane(b, c0) + 1]
            return bass.AP(tensor=base.tensor, offset=base.offset,
                           ap=[list(base.ap[0]), [P + 1, c1 - c0], [P, S]])

        SMALL_ALL = 16 * 9
        CONSTS = 6
        SIGN_LAG = 4
        def slot_tile(n):
            return n // (2 * KS), n % 2, n // 2 % KS

        block = stack.enter_context(nc.Block())

        @block.sync
        def _(sp):
            sp.wait_ge(zeroed, 1)
            for h in range(2):
                sp.dma_start(x_s[SP * h:SP * h + S, :, :],
                             x[h::2, :, :].rearrange("t s d -> s t d")).then_inc(x_in, 16)
            for b in range(B):
                src = ctx_in[b, :, :].rearrange("(c p) d -> p c d", p=N)
                size = C // len(ctx_part[b])
                for j, part in enumerate(ctx_part[b]):
                    for p0, p1 in ((0, 96), (96, N)):
                        sp.dma_start(ctx_n[p0:p1, C * b + size * j:C * b + size * (j + 1), :],
                                     src[p0:p1, size * j:size * (j + 1), :]).then_inc(part, 16)
                if b == 1:
                    sp.dma_start(se_n[:, :, :], slot_embeds.rearrange("e t d -> (e t) d").rearrange("(k p) d -> p k d", p=P))\
                       .then_inc(se_in, 16)
            sp.dma_start(w1_s[:, :], w1).then_inc(w12_in, 16)
            sp.dma_start(w2_s[:, :, :], w2.rearrange("(q p) d -> p q d", p=P)).then_inc(w12_in, 16)
            sp.dma_start(gx_b[:, :], g_xattn.unsqueeze(0).to_broadcast([P, 2])).then_inc(g_in, 16)
            sp.dma_start(gf_b[:, :], g_ffn.unsqueeze(0).to_broadcast([P, 2])).then_inc(g_in, 16)
            for dst, src in (
                (wc_n[:, :, :], Wc.rearrange("e (h d) -> e h d", h=2)),
                (b1_n[:, :], eb1.rearrange("e (q p) -> (e q) p", p=P)),
                (gam_x[:, :], gamma_x.unsqueeze(1)),
                (gam_s[:, :], gamma_slot.unsqueeze(1)),
                (bc_s[:, :], bc.unsqueeze(0)),
                (b2_s[:, :], eb2),
                (gw_s[:, :], gate_w),
                (gb_b[:, :], gate_b.unsqueeze(0).to_broadcast([P, E])),
                (temp_s[:, :], temperature.unsqueeze(0).to_broadcast([P, 1])),
            ):
                sp.dma_start(dst, src).then_inc(small_in, 16)
            sp.wait_ge(prod_ps, 2 * B)
            sp.dma_start(ew1_s, eW1.rearrange("e d f -> d e f")).then_inc(ew1_in, 16)
            sp.wait_ge(flags_up, 2 * STEPS)
            sp.wait_ge(gap2_up, NSP - 1)
            sp.wait_ge(last_flags, 1)
            sp.dma_start(ew2_s, eW2.rearrange("e (q p) d -> p e q d", p=P)).then_inc(ew2_in, 16)
            for t in range(0, TT, 2):
                sp.wait_ge(fin_up, t + 2)
                for h in range(2):
                    sp.dma_start(out[2 * t + h:2 * t + 4:2, :, :].rearrange("t s d -> s t d"),
                                 x_s[SP * h:SP * h + S, t:t + 2, :]).then_inc(out_done, 16)
            sp.wait_ge(out_done, 16 * TT)

        @block.gpsimd
        def _(pool):
            g = nc.gpsimd
            g.memset(eps[:, :], LN_EPS).then_inc(consts, 1)
            g.memset(ident[:, :], 0.0).then_inc(consts, 1)
            g.memset(ones[:, :], 1.0).then_inc(consts, 1)
            pool.wait_ge(consts, 3)
            g.affine_select(out=ident[:, :], in_=ident[:, :], compare_op=ALU.not_equal, fill=1.0, base=0,
                            pattern=[[-1, P]], channel_multiplier=1).then_inc(consts, 1)
            g.iota(lane_i[:, :], pattern=[[0, 1]], base=0, channel_multiplier=1).then_inc(consts, 1)
            g.iota(key_row[:, :], pattern=[[4, N]], base=4 - 4 * N, channel_multiplier=0,
                   allow_small_or_imprecise_dtypes=True).then_inc(consts, 1)
            g.memset(prod[:, 0:C - 1, :], PAD_D2).then_inc(pads, 1)
            g.memset(prod[:, S:STEPS, :], PAD_D2).then_inc(pads, 1)
            g.memset(prod[:, C - 1:S, 0:P:LPB], PAD_D2).then_inc(pads, 1)
            g.memset(turn[:, :], 0.0).then_inc(pads, 1)
            g.memset(tiny[:, :], TINY).then_inc(pads2, 1)
            g.memset(lane_sel[:, :], 0.0).then_inc(pads, 1)
            pool.wait_ge(pads, 5)
            g.affine_select(out=turn[:, :], in_=turn[:, :], compare_op=ALU.not_equal, fill=1.0, base=0,
                            pattern=[[-1, N]], channel_multiplier=1).then_inc(pads, 1)
            pool.wait_ge(pads, 6)
            g.affine_select(out=turn[:, :], in_=turn[:, :], compare_op=ALU.not_equal, fill=1.0, base=-N,
                            pattern=[[0, N]], channel_multiplier=1).then_inc(pads, 1)
            g.affine_select(out=lane_sel[:, :], in_=lane_sel[:, :], compare_op=ALU.not_equal, fill=1.0,
                            base=-1, pattern=[[-LPB, B]], channel_multiplier=1).then_inc(pads2, 1)
            g.iota(row4[:, :], pattern=[[4 * N, C]], base=4, channel_multiplier=4,
                   allow_small_or_imprecise_dtypes=True).then_inc(pads2, 1)
            g.iota(row4b[:, :], pattern=[[4 * N, C]], base=6, channel_multiplier=4,
                   allow_small_or_imprecise_dtypes=True).then_inc(pads2, 1)
            g.iota(e_iota[:, :], pattern=[[1, E]], base=0, channel_multiplier=0,
                   allow_small_or_imprecise_dtypes=True).then_inc(pads2, 1)
            for b in range(B):
                for part in ctx_part[b]:
                    pool.wait_ge(part, 32)
                if b >= 2:
                    pool.wait_ge(aa_pool, b - 1)
                if b >= 1:
                    pool.wait_ge(sq_up, b)
                rows = ctx_n[0:N, C * b + ACT_SQ:C * b + ACT_SQ + POOL_SQ, :]
                g.tensor_tensor(squares[0:N, b % 2, :, :], rows, rows, ALU.mult).then_inc(sq_up, 1)
            pool.wait_ge(prod_ps, 2 * B)
            for s0, s1 in SPANS:
                rows = cost[:, s0:s1, :]
                pool.wait_ge(wave_r, s1 - 1)
                g.tensor_tensor(key_t[:, s0:s1, 1:R], rows[:, :, 0:N], rows[:, :, 1:R],
                                ALU.subtract).then_inc(gap_up, 1)
                if s1 == STEPS:
                    break
                pool.wait_ge(wave_r, s1)
                g.tensor_tensor(diag_f[:, s0:s1, :], cost[:, s0 + 1:s1 + 1, 0:N], rows[:, :, 0:N],
                                ALU.subtract).then_inc(gap2_up, 1)
            pool.wait_ge(key_up, NSP)
            for n in range(NSP - 2, -1, -1):
                s0, s1 = SPANS[n]
                rows = key_t[:, s0:s1, 1:R]
                g.tensor_tensor(rows, rows, key4[:, None, :].to_broadcast([P, s1 - s0, N]),
                                ALU.mult).then_inc(scaled_up, 1)
                pool.wait_ge(scaled_up, NSP - 1 - n)
                pool.wait_ge(merge_up, 2 if n == NSP - 2 else NMERGE + max(0, AHEAD_S - s0))
                g.tensor_tensor(rows, rows, left_f[:, s0:s1, :], ALU.mult).then_inc(picked_up, 1)
            pool.wait_ge(picked_up, NSP - 1)
            g.memset(mask[0:N, :, :, S:SP], 0.0).then_inc(pads2, 1)
            pool.wait_ge(exp_ps, TT)
            g.memset(disp_e[:, :, :, S:SP], 0.0).then_inc(pads2, 1)
            g.memset(y_t.rearrange("p q (b s) -> p q b s", b=B)[:, :, :, S:SP], 0.0).then_inc(pads2, 1)
            pool.wait_ge(hy_used, B * KS)
            g.memset(ht_s.rearrange("p r q (b s) -> p (r q b) s", b=B)[:, :, S:SP], 0.0).then_inc(pads2, 1)

        @block.scalar
        def _(act):
            a = nc.scalar

            def roots(n, h):
                pair = slice(2 * h, 2 * h + 2)
                act.wait_ge(var_up, 4 * (n - 1) + 2 * h + 2)
                if n == 2:
                    a.activation(vr[:, 0, pair], mv[:, pair, 1], ACT.Sqrt)
                a.activation(vr[:, 1, pair], mv[:, pair, 1], ACT.Sqrt, bias=eps[:, 0:1]).then_inc(root_up, 1)

            def tokens_out(n, t, scale=1.0):
                act.wait_ge(xt_ps, TT * (n - 1) + t + 1)
                a.activation(xt_s[:, t * P:(t + 1) * P], bank(XT_BANKS[n][t])[:, 0:P], ACT.Copy,
                             scale=scale).then_inc(xt_up, 1)

            act.wait_ge(consts, 1)
            roots(1, 0)
            roots(1, 1)
            nsq = [0]

            def context_out(k):
                act.wait_ge(ctx_ps, k + 1)
                a.activation(region_x[:, k * TG * N:(k + 1) * TG * N], bank(k % 3)[:, 0:TG * N], ACT.Copy,
                             accum_out=csum_g[:, k // GPB, k % GPB:k % GPB + 1]).then_inc(ctx_up, 1)

            def norms(b, chunks):
                for c in chunks:
                    if nsq[0] >= 2:
                        act.wait_ge(aa_act, nsq[0] - 1)
                    a.activation(junk_a[0:N, nsq[0] % 2, :], ctx_n[0:N, C * b + c, :], ACT.Square,
                                 accum_out=aa_n[0:N, lane(b, c):lane(b, c) + 1]).then_inc(aa_act, 1)
                    nsq[0] += 1

            for k in range(GPB):
                context_out(k)
            act.wait_ge(xt_ps, TT)
            a.activation(xt_s[:, :], bank(6), ACT.Copy, scale=-2.0).then_inc(xt_up, 1)
            a.activation(xsq_s[:, :], bank(6), ACT.Square).then_inc(xt_up, 1)
            norms(0, range(2))
            context_out(GPB)
            act.wait_ge(bb_ps, 1)
            a.activation(bb_s[:, :, :].rearrange("p b s -> p (b s)"), bank(6), ACT.Copy).then_inc(bb_up, 1)
            norms(0, range(2, ACT_SQ))
            norms(1, range(0, ACT_SQ, GPB))
            for k in range(GPB + 1, NG):
                context_out(k)
                norms(k // GPB, range(k % GPB, ACT_SQ, GPB))
                if k == 3 * GPB - 1:
                    act.wait_ge(se_sum, 1)
                    a.activation(se_r[:, :], se_r[:, :], ACT.Sqrt).then_inc(se_root, 1)
            for n in range(SIGN_LAG + NSP):
                if n < ND:
                    act.wait_ge(dist_ps, n + 1)
                    if n == 0:
                        act.wait_ge(aa_pool, B)
                    s0, s1 = DSPANS[n]
                    rows = cost[:, 1 + s0:1 + s1, 1:R]
                    a.activation(rows, bank(n % 3)[:, 0:(s1 - s0) * N].rearrange("p (s n) -> p s n", n=N),
                                 ACT.Relu).then_inc(relu_up, 1)
                    act.wait_ge(relu_up, n + 1)
                    a.activation(rows, rows, ACT.Sqrt).then_inc(dist_up, 1)
                if n >= SIGN_LAG:
                    m = n - SIGN_LAG
                    s0, s1 = SPANS[m]
                    act.wait_ge(gap_up, m + 1)
                    rows = key_t[:, s0:s1, 1:R]
                    a.activation(rows, rows, ACT.Sign).then_inc(sign_up, 1)
                    act.wait_ge(sign_up, m + 1)
                    a.activation(rows, rows, ACT.Copy, scale=SIDE, bias=1.0).then_inc(key_up, 1)
                    if s1 == STEPS:
                        break
                    act.wait_ge(gap2_up, m + 1)
                    rows = diag_f[:, s0:s1, :]
                    a.activation(rows, rows, ACT.Sign, bias=tiny[:, 0:1]).then_inc(flags_d, 1)
                if n == SMALL_AT:
                    act.wait_ge(small_ps, 1)
                    a.activation(wc_t[:, :, :].rearrange("p h d -> p (h d)"), bank(7)[:, 0:2 * D], ACT.Copy).then_inc(small_up, 1)
                    a.activation(b1_t[:, :], bank(7)[:, 2 * D:2 * D + E * Q], ACT.Copy).then_inc(small_up, 1)
                    act.wait_ge(small_ps, 2)
                    a.activation(se_t[:, :], bank(5), ACT.Copy, scale=gam_s[:, 0:1]).then_inc(small_up, 1)
            act.wait_ge(keys_up, STEPS - KEYS_A + 1)
            for b in range(B):
                last = a.activation(keys_x[:, b, KEYS_A:S + 1], keys[:, KEYS_A:S + 1], ACT.Copy,
                                    scale=lane_sel[:, b:b + 1])
            last.then_inc(keys_a, 1)
            act.wait_ge(g_in, 32)
            a.activation(tgx[:, :], gx_b[:, :], ACT.Tanh).then_inc(tg_up, 1)
            a.activation(tgf[:, :], gf_b[:, :], ACT.Tanh).then_inc(tg_up, 1)
            roots(2, 0)
            tokens_out(2, 0, gam_x[:, 0:1])
            tokens_out(2, 1, gam_x[:, 0:1])
            roots(2, 1)

            def xw_out(t):
                act.wait_ge(xw_ps, t + 1)
                a.activation(xw_s[:, t, :], bank(1 + t), ACT.Copy).then_inc(xw_up, 1)

            xw_out(0)
            xw_out(1)
            tokens_out(2, 2, gam_x[:, 0:1])
            tokens_out(2, 3, gam_x[:, 0:1])
            for k in range(KS):
                act.wait_ge(ld_sub, k + 1)
                a.activation(disp_e[:, k, :, 0:S], disp_e[:, k, :, 0:S], ACT.Exp).then_inc(ld_exp, 1)
                if k < 2:
                    xw_out(2 + k)
            for t in range(TT):
                act.wait_ge(lc_max, t + 1)
                a.activation(comb_e[:, t, :], bank(1 + t), ACT.Exp, bias=c_nmax[:, t:t + 1],
                             accum_out=c_sum[:, t:t + 1]).then_inc(lc_exp, 1)
            for t in range(TT):
                act.wait_ge(disp_ps, t + 1)
                a.activation(disp_t[:, t, :], bank(XT_BANKS[2][t]), ACT.Copy).then_inc(disp_up, 1)
            act.wait_ge(d_inv_up, 1)
            for n in range(B * KS):
                t, h, k = slot_tile(n)
                act.wait_ge(h_ps, n + 1)
                if n >= NHR:
                    act.wait_ge(hy_used, n - NHR + 1)
                a.activation(h_s[:, n % NHR, :], bank(H_BANKS[n % 4]), ACT.Gelu,
                             scale=d_inv[:, k, 2 * t + h:2 * t + h + 1]).then_inc(h_up, 1)
            for h in range(2):
                roots(3, h)
            for t in range(TT):
                tokens_out(3, t)
            for h in range(2):
                roots(4, h)
            for t in range(TT):
                tokens_out(4, t)
            for n in range(E * Q):
                e, q = divmod(n, Q)
                if n == 2 * Q:
                    act.wait_ge(gd_up, 1)
                    a.activation(gexp[:, :], gdiff[:, :], ACT.Exp).then_inc(ge_up, 1)
                act.wait_ge(eh_ps, n + 1)
                if n == 0:
                    act.wait_ge(pads2, 9)
                if e >= 2 and q == 0:
                    act.wait_ge(eo_ps, e - 1)
                a.activation(tokens(ht_s[:, e % 2, q, :]), bank(n % 3)[:, 0:B * S].rearrange("p (b s) -> p b s", b=B),
                             ACT.Gelu, bias=b1_t[:, n:n + 1]).then_inc(eh_up, 1)

        @block.tensor
        def _(pe):
            T = nc.tensor
            pe.wait_ge(consts, 4)

            def keep_warm(times, free_bank=7):
                for _ in range(times):
                    T.matmul(bank(free_bank)[:, 0:P], ones[:, :], ident[:, :], start=True, stop=True)

            def transpose_tokens(n, t):
                pe.wait_ge(xn_up, TT * (n - 1) + t + 1)
                to, at = (6, t * P) if n == 1 else (XT_BANKS[n][t], 0)
                T.transpose(bank(to)[:, at:at + P], xn_s[:, t, :], ident[:, :]).then_inc(xt_ps, 1)

            def query_norms():
                pe.wait_ge(xt_up, 2)
                T.matmul(bank(6), ones[:, :], xsq_s[:, :], start=True, stop=True).then_inc(bb_ps, 1)

            def transpose_ctx(k):
                pe.wait_ge(ctx_part[0][k] if k < GPB else ctx_part[k // GPB][0], 32)
                if k >= 3:
                    pe.wait_ge(ctx_up, k - 2)
                for i in range(TG):
                    last = T.transpose(bank(k % 3)[:, i * N:(i + 1) * N], ctx_n[0:N, TG * k + i, :],
                                       ident[0:N, 0:N])
                last.then_inc(ctx_ps, 1)

            def products(n):
                b, h = divmod(n, 2)
                c0, c1 = HALVES[h]
                pe.wait_ge(ctx_up, GPB * b + (c1 + TG - 1) // TG)
                if n >= 3:
                    pe.wait_ge(prod_up, n - 2)
                for c in range(c0, c1):
                    last = T.matmul(bank(3 + n % 3)[0:N, (c - c0) * S:(c - c0 + 1) * S], ctx_t[:, C * b + c, :],
                                    xt_s[:, SP * b:SP * b + S], start=True, stop=True)
                last.then_inc(prod_ps, 1)

            def weights_by_feature():
                pe.wait_ge(small_in, SMALL_ALL)
                for h in range(2):
                    T.transpose(bank(7)[:, h * D:(h + 1) * D], wc_n[:, h, :], ident[:, :])
                T.transpose(bank(7)[:, 2 * D:2 * D + E * Q], b1_n[:, :], ident[0:E * Q, 0:E * Q]).then_inc(small_ps, 1)
                pe.wait_ge(se_up, KS)
                pe.wait_ge(prod_up, 2 * B)
                for k in range(KS):
                    last = T.transpose(bank(5)[:, k * P:(k + 1) * P], se_n[:, k, :], ident[:, :])
                last.then_inc(small_ps, 1)

            keep_warm(START_WARM)
            for k in range(GPB):
                transpose_ctx(k)
            for t in range(TT):
                transpose_tokens(1, t)
            pe.wait_ge(xt_up, 1)
            for b in range(1, B):
                transpose_ctx(GPB * b)
                products(2 * b - 2)
                if b == 1:
                    query_norms()
                transpose_ctx(GPB * b + 1)
                products(2 * b - 1)
                transpose_ctx(GPB * b + 2)
            products(2 * B - 2)
            products(2 * B - 1)
            pe.wait_ge(prod_up, 2 * B)
            pe.wait_ge(pads, 7)
            for n in range(ND):
                if n >= 3:
                    pe.wait_ge(relu_up, n - 2)
                s0, s1 = DSPANS[n]
                for s in range(s0, s1):
                    last = T.matmul(bank(n % 3)[:, (s - s0) * N:(s - s0 + 1) * N], prod[0:R, s, :], turn[0:R, :],
                                    start=True, stop=True)
                last.then_inc(dist_ps, 1)
                if n == SMALL_AT:
                    weights_by_feature()
            pe.wait_ge(relu_up, ND)
            pe.wait_ge(keys_a, 1)
            T.matmul(keys_b[0:N, :, KEYS_A:S + 1], ones[:, 0:N], keys_x[:, :, KEYS_A:S + 1], start=True, stop=True)
            pe.wait_ge(small_up, 3)
            pe.wait_ge(keys_up, STEPS - WARM_AT)
            keep_warm(KEYS_WARM)
            pe.wait_ge(keys_z, 1)
            T.matmul(keys_b[0:N, :, 0:KEYS_A], ones[:, 0:N], keys_x[:, :, 0:KEYS_A],
                     start=True, stop=True).then_inc(kb_ps, 1)
            keep_warm(MASK_WARM)
            pairs = ctx_n[0:N, :, :].rearrange("p (t h c) d -> p t h c d", h=2, c=C)
            def aligned(t, c):
                return T.matmul(bank(1 + t)[:, 0:2 * D], mask[0:N, c, 2 * t:2 * t + 2, :].rearrange("p h s -> p (h s)"),
                                pairs[:, t, :, c, :], start=(c == 0), stop=(c == C - 1))

            for c in range(C - TAIL_C):
                pe.wait_ge(mask_up, c + 1)
                for t in range(TT):
                    aligned(t, c)
            pe.wait_ge(mask_up, C)
            for t in range(TT):
                for c in range(C - TAIL_C, C):
                    last = aligned(t, c)
                last.then_inc(exp_ps, 1)

            pe.wait_ge(w12_in, 32)

            def xw_product(t):
                pe.wait_ge(xt_up, 2 + t + 1)
                T.matmul(bank(1 + t), xt_s[:, t * P:(t + 1) * P], w1_s[:, :], start=True, stop=True).then_inc(xw_ps, 1)

            keep_warm(NORM_WARM[0])
            for h in range(2):
                transpose_tokens(2, 2 * h)
                transpose_tokens(2, 2 * h + 1)
                if h == 0:
                    xw_product(0)
                    xw_product(1)
            pe.wait_ge(small_up, 3)
            pe.wait_ge(xt_up, 2 + TT)
            for k in range(KS):
                T.matmul(bank(XT_BANKS[2][k])[:, 0:B * S], se_t[:, k * P:(k + 1) * P], tokens(xt_s[:, :]),
                         start=True, stop=True).then_inc(ld_ps, 1)
            xw_product(2)
            xw_product(3)
            for t in range(TT):
                pe.wait_ge(xw_up, t + 1)
                T.matmul(bank(1 + t), xt_s[:, t * P:(t + 1) * P], se_t[:, :], start=True, stop=True).then_inc(lc_ps, 1)
            pe.wait_ge(ld_exp, KS)
            pe.wait_ge(pads2, 7)
            for t in range(TT):
                for k in range(KS):
                    last = T.transpose(bank(XT_BANKS[2][t])[:, k * P:(k + 1) * P],
                                       disp_e[:, k, 2 * t:2 * t + 2, :].rearrange("p h s -> p (h s)"), ident[:, :])
                last.then_inc(disp_ps, 1)
            pe.wait_ge(lc_exp, TT)
            for k in range(KS):
                for t in range(TT):
                    last = T.transpose(bank(1 + k)[:, t * P:(t + 1) * P], comb_e[:, t, k * P:(k + 1) * P], ident[:, :])
                last.then_inc(comb_ps, 1)

            def hidden(n):
                t, h, k = slot_tile(n)
                if k == 0 and h == 0:
                    pe.wait_ge(disp_up, TT if n == 0 else t + 1)
                if n == 3:
                    pe.wait_ge(comb_up, KS)
                if n >= 4:
                    pe.wait_ge(h_up, n - 3)
                T.matmul(bank(H_BANKS[n % 4]), disp_t[SP * h:SP * h + S, t, k * P:(k + 1) * P],
                         xw_s[SP * h:SP * h + S, t, :], start=True, stop=True).then_inc(h_ps, 1)

            def combined(n):
                t, h, k = slot_tile(n)
                pe.wait_ge(h_up, n + 1)
                if k == 0:
                    pe.wait_ge(comb_up, KS)
                    if t >= 1:
                        pe.wait_ge(y_up, 2 * t - 1 + h)
                at = SP * (2 * t + h)
                for q in range(Q):
                    last = T.matmul(bank(h)[:, q * S:(q + 1) * S], h_s[:, n % NHR, q * P:(q + 1) * P],
                                    comb_t[:, k, at:at + S], start=(k == 0 and q == 0), stop=(k == KS - 1),
                                    skip_group_check=True)
                last.then_inc(hy_used, 1)

            pe.wait_ge(xw_up, TT)

            def second_layer(t):
                pe.wait_ge(y_up, 2 * t + 2)
                if t == 0:
                    pe.wait_ge(pads2, 8)
                if t >= 2:
                    pe.wait_ge(f0_used, t - 1)
                for q in range(Q):
                    last = T.matmul(bank(2 + t % 2)[:, 0:D], y_t[:, q, t * P:(t + 1) * P], w2_s[:, q, :],
                                    start=(q == 0), stop=(q == Q - 1))
                last.then_inc(f0_ps, 1)

            for n in range(0, B * KS + 2, 2):
                if n < B * KS:
                    hidden(n)
                    hidden(n + 1)
                if n >= 2:
                    combined(n - 2)
                    combined(n - 1)
                    t = (n - 2) // (2 * KS) - 1
                    if t >= 0 and (n - 2) % (2 * KS) == 0:
                        second_layer(t)

            def mean_and_bias(t):
                dst = bank(4 + t)[:, 0:D]
                T.matmul(dst, csum_b[:, 2 * t:2 * t + 2, :].rearrange("p h s -> p (h s)"), wc_t[:, 1, :],
                         start=True, stop=False)
                T.matmul(dst, ones[0:1, :], bc_s[0:1, :], start=False, stop=False)

            def token_part(t):
                pe.wait_ge(xt_up, 2 + TT + t + 1)
                T.matmul(bank(4 + t)[:, 0:D], xt_s[:, t * P:(t + 1) * P], wc_t[:, 0, :],
                         start=False, stop=True).then_inc(xa_ps, 1)

            pe.wait_ge(small_up, 2)
            pe.wait_ge(csum_up, 1)
            mean_and_bias(0)
            mean_and_bias(1)
            second_layer(TT - 1)
            transpose_tokens(3, 0)
            transpose_tokens(3, 1)
            mean_and_bias(2)
            mean_and_bias(3)
            token_part(0)
            token_part(1)
            keep_warm(NORM_WARM[1], 0)
            transpose_tokens(3, 2)
            transpose_tokens(3, 3)
            token_part(2)
            token_part(3)

            keep_warm(NORM_WARM[2], 0)
            for t in range(TT):
                transpose_tokens(4, t)
            pe.wait_ge(xt_up, 2 + 3 * TT)
            def expert_hidden(e):
                if e == 0:
                    pe.wait_ge(ew1_in, 16)
                for q in range(Q):
                    n = e * Q + q
                    if n >= 3:
                        pe.wait_ge(eh_up, n - 2)
                    T.matmul(bank(n % 3)[:, 0:B * S], ew1_s[:, e, q * P:(q + 1) * P], tokens(xt_s[:, :]),
                             start=True, stop=True).then_inc(eh_ps, 1)

            def expert_out(e):
                if e == 0:
                    pe.wait_ge(ew2_in, 16)
                if e >= 2:
                    pe.wait_ge(eo_up, TT * (e - 1))
                pe.wait_ge(eh_up, Q * (e + 1))
                for t in range(TT):
                    dst = bank(LAST_BANKS[t])[:, 0:D] if e == E - 1 else bank(4 + e % 2)[:, t * D:(t + 1) * D]
                    for q in range(Q):
                        last = T.matmul(dst, ht_s[:, e % 2, q, t * P:(t + 1) * P], ew2_s[:, e, q, :],
                                        start=(q == 0), stop=(q == Q - 1))
                    if e == E - 1 or t == TT - 1:
                        last.then_inc(eo_ps, 1)

            def weights_by_expert():
                pe.wait_ge(wt_up, 1)
                for t in range(TT):
                    last = T.transpose(bank(7)[0:E, t * P:(t + 1) * P], wt[:, t, :], ident[:, :])
                last.then_inc(wtt_ps, 1)

            def second_biases():
                pe.wait_ge(wtt_up, 1)
                for t in range(TT):
                    last = T.matmul(bank(3)[:, t * D:(t + 1) * D], wt_t[:, t * P:(t + 1) * P], b2_s[:, :],
                                    start=True, stop=True)
                last.then_inc(b2_ps, 1)

            def gate_logits():
                for t in range(TT):
                    dst = bank(6)[:, t * E:(t + 1) * E]
                    last = T.matmul(dst, xt_s[:, t * P:(t + 1) * P], gw_s[:, :], start=True, stop=True)
                last.then_inc(g_ps, 1)

            expert_hidden(0)
            gate_logits()
            for e in range(E):
                if e + 1 < E:
                    expert_hidden(e + 1)
                if e == 1:
                    weights_by_expert()
                expert_out(e)
                if e == 1:
                    second_biases()

        @block.vector
        def _(dve):
            v = nc.vector
            done = [0]

            def link(ins):
                done[0] += 1
                ins.then_inc(dve_c, 1)
                dve.wait_ge(dve_c, done[0])

            def mark(ins):
                done[0] += 1
                ins.then_inc(dve_c, 1)

            def variances(h):
                pair = (2 * h, 2 * h + 1)
                dve.wait_ge(dve_c, done[0])
                for t in pair:
                    mark(v.bn_stats(stats[:, t, :], x_s[:, t, :]))
                dve.wait_ge(dve_c, done[0])
                for t in pair:
                    v.bn_aggr(mv[:, t, :], stats[:, t, :]).then_inc(var_up, 1)

            def normalise(n, h):
                pair = slice(2 * h, 2 * h + 2)
                dve.wait_ge(root_up, 2 * (n - 1) + h + 1)
                dve.wait_ge(var_up, 4 * (n - 1) + 2 * h + 2)
                if n == 2:
                    link(v.scalar_tensor_tensor(den[:, pair], vr[:, 1, pair], RMS_EPS / D ** 0.5, vr[:, 0, pair],
                                                ALU.mult, ALU.max))
                    link(v.reciprocal(fac[:, pair], den[:, pair]))
                else:
                    link(v.reciprocal(fac[:, pair], vr[:, 1, pair]))
                for t in (2 * h, 2 * h + 1):
                    v.tensor_scalar(xn_s[:, t, :], x_s[:, t, :], mv[:, t, 0:1], fac[:, t:t + 1],
                                    ALU.subtract, ALU.mult).then_inc(xn_up, 1)

            v.memset(x_s[:, :, :], 0.0).then_inc(zeroed, 1)
            dve.wait_ge(consts, CONSTS)
            link(v.tensor_scalar(lane_m[:, :], lane_i[:, :], LPB - 1, None, ALU.bitwise_and))
            link(v.tensor_copy(lane_f[:, :], lane_m[:, :]))
            link(v.tensor_scalar(lane4[:, :], lane_f[:, :], 4.0 * N, None, ALU.mult))
            mark(v.memset(cost[:, 0, :], INF))
            link(v.tensor_scalar(key4[:, :], key_row[:, :], lane4[:, 0:1], None, ALU.add))
            link(v.tensor_scalar(lane0[:, :], lane_f[:, :], 1.0, -INF, ALU.is_equal, ALU.mult))
            link(v.tensor_scalar(cost[:, 0, 0:1], lane0[:, :], INF, None, ALU.add))
            v.tensor_scalar(keys[:, STEPS:STEPS + 1], lane_f[:, :], 0.0, float(LAST_KEY),
                            ALU.is_gt, ALU.mult).then_inc(keys_up, 1)

            dve.wait_ge(x_in, 32)
            variances(0)
            variances(1)
            normalise(1, 0)
            normalise(1, 1)

            nsq = [0]

            def square_sums(b):
                for part in ctx_part[b]:
                    dve.wait_ge(part, 32)
                for c in range(ACT_SQ + POOL_SQ, C):
                    if nsq[0] >= 2:
                        dve.wait_ge(aa_up, nsq[0] - 1)
                    v.tensor_tensor_reduce(junk_v[0:N, nsq[0] % 2, :], ctx_n[0:N, C * b + c, :],
                                           ctx_n[0:N, C * b + c, :], 1.0, 0.0, ALU.mult, ALU.add,
                                           aa_n[0:N, lane(b, c):lane(b, c) + 1]).then_inc(aa_up, 1)
                    nsq[0] += 1

            def store_products(b):
                dve.wait_ge(bb_rows, b + 1)
                dve.wait_ge(aa_act, ACT_SQ * (b + 1))
                dve.wait_ge(aa_up, (C - ACT_SQ - POOL_SQ) * (b + 1))
                dve.wait_ge(aa_pool, b + 1)
                for h, (c0, c1) in enumerate(HALVES):
                    n = 2 * b + h
                    dve.wait_ge(prod_ps, n + 1)
                    v.tensor_tensor(diagonal(b, c0, c1, 0, N),
                                    bank(3 + n % 3)[0:N, 0:(c1 - c0) * S].rearrange("p (c s) -> p c s", s=S),
                                    aa_n[0:N, lane(b, c0):lane(b, c1), None].to_broadcast([N, c1 - c0, S]),
                                    ALU.add).then_inc(prod_up, 1)

            def add_squares(b):
                dve.wait_ge(sq_up, b + 1)
                v.tensor_reduce(aa_n[0:N, lane(b, ACT_SQ):lane(b, ACT_SQ + POOL_SQ)], squares[0:N, b % 2, :, :],
                                AX.X, ALU.add).then_inc(aa_pool, 1)

            def norm_rows(b):
                if b == 0:
                    dve.wait_ge(bb_up, 1)
                    dve.wait_ge(pads, 5)
                v.tensor_copy(diagonal(b, 0, C, QUARTER, R),
                              bb_s[QUARTER:R, b:b + 1, 0:S].to_broadcast([R - QUARTER, C, S])).then_inc(bb_rows, 1)

            def slot_sums():
                dve.wait_ge(se_in, 16)
                for k in range(KS):
                    if k >= 2:
                        dve.wait_ge(dve_c, done[0] - 1)
                    mark(v.tensor_tensor_reduce(junk_v[:, k % 2, :], se_n[:, k, :], se_n[:, k, :], 1.0, 0.0,
                                                ALU.mult, ALU.add, se_sq[:, k:k + 1]))
                dve.wait_ge(dve_c, done[0])
                v.tensor_scalar(se_r[:, :], se_sq[:, :], 1.0 / D, None, ALU.mult).then_inc(se_sum, 1)

            def slots_normalised():
                dve.wait_ge(se_root, 1)
                link(v.tensor_scalar(se_r[:, :], se_r[:, :], RMS_EPS / D ** 0.5, None, ALU.max))
                link(v.reciprocal(se_r[:, :], se_r[:, :]))
                for k in range(KS):
                    v.tensor_scalar(se_n[:, k, :], se_n[:, k, :], se_r[:, k:k + 1], None, ALU.mult).then_inc(se_up, 1)

            square_sums(0)
            norm_rows(0)
            for b in range(1, B):
                square_sums(b)
                add_squares(b - 1)
                norm_rows(b)
                store_products(b - 1)
                if b == 2:
                    slot_sums()
                if b == 4:
                    slots_normalised()
            add_squares(B - 1)
            store_products(B - 1)

            from_above = [i if i % LPB == 0 else i - 1 for i in range(32)]

            def flag_left(s, h):
                v.tensor_tensor(left_f[:, s, N // 2 * h:N // 2 * (h + 1)], cost[:, s, 1 + N // 2 * h:1 + N // 2 * (h + 1)],
                                cost[:, s + 1, N // 2 * h:N // 2 * (h + 1)], ALU.is_lt).then_inc(flags_up, 1)

            for s in range(STEPS):
                if s >= 1:
                    dve.wait_ge(wave_r, s)
                v.stream_shuffle(cost[:, s + 1, 0:1], cost[:, s, N:R], from_above)
                v.tensor_tensor(m_s[:, s % 2, :], cost[:, s, 1:R], cost[:, s, 0:N], ALU.min).then_inc(wave_m, 1)
                if s >= 1:
                    flag_left(s - 1, 0)
                for n in range(ND):
                    if s == DSPANS[n][0]:
                        dve.wait_ge(dist_up, n + 1)
                dve.wait_ge(wave_m, s + 1)
                v.tensor_tensor_scan(cost[:, s + 1, 1:R], m_s[:, s % 2, :], cost[:, s + 1, 1:R],
                                     cost[:, s + 1, 0:1], ALU.min, ALU.add).then_inc(wave_r, 1)
                if s >= 1:
                    flag_left(s - 1, 1)
            dve.wait_ge(wave_r, STEPS)
            flag_left(STEPS - 1, 0)
            flag_left(STEPS - 1, 1)
            s0, s1 = SPANS[-1]
            v.tensor_tensor(diag_f[:, s0:s1, :], cost[:, s0:s1, 0:N], cost[:, s0 + 1:s1 + 1, 0:N],
                            ALU.is_le).then_inc(last_flags, 1)
            v.memset(below[:, :, 0:1], 1.0)
            dve.wait_ge(flags_up, 2 * STEPS)
            dve.wait_ge(last_flags, 1)

            from_below = [i if i % LPB == 0 else (i + 1) % 32 for i in range(32)]

            def merge_flags(s0, s1):
                rows = left_f[:, s0:s1, :]
                v.tensor_tensor(rows, rows, diag_f[:, s0:s1, :], ALU.max).then_inc(merge_up, 1)

            merge_flags(s0, s1)
            rows = key_t[:, s0:s1, 1:R]
            dve.wait_ge(key_up, NSP)
            link(v.tensor_tensor(rows, rows, key4[:, None, :].to_broadcast([P, s1 - s0, N]), ALU.mult))
            dve.wait_ge(merge_up, 1)
            link(v.tensor_tensor(rows, rows, left_f[:, s0:s1, :], ALU.mult))
            dve.wait_ge(flags_d, NSP - 1)
            merge_flags(*SPANS[NSP - 2])
            for s in range(STEPS - 1, -1, -1):
                i = STEPS - 1 - s
                dve.wait_ge(keys_up, i + 1)
                v.stream_shuffle(key_t[:, s, 0:1], keys[:, s + 1:s + 2], from_below)
                v.tensor_scalar(below[:, i % 2, 1:R], key4[:, :], keys[:, s + 1:s + 2], None,
                                ALU.is_lt).then_inc(below_up, 1)
                if i == 0:
                    merge_flags(*SPANS[NSP - 3])
                elif i <= AHEAD_S:
                    merge_flags(AHEAD_S - i, AHEAD_S - i + 1)
                for n in range(NSP - 1):
                    if s == SPANS[n][1] - 1:
                        dve.wait_ge(picked_up, NSP - 1 - n)
                dve.wait_ge(below_up, i + 1)
                v.tensor_tensor_reduce(hit[:, i % 2, :], below[:, i % 2, :], key_t[:, s, :], 1.0, 0.0,
                                       ALU.mult, ALU.max, keys[:, s:s + 1]).then_inc(keys_up, 1)

            dve.wait_ge(keys_up, STEPS + 1)
            v.tensor_tensor(keys_x[:, :, 0:KEYS_A], keys[:, None, 0:KEYS_A].to_broadcast([P, B, KEYS_A]),
                            lane_sel[:, :, None].to_broadcast([P, B, KEYS_A]), ALU.mult).then_inc(keys_z, 1)
            dve.wait_ge(pads2, 6)
            dve.wait_ge(kb_ps, 1)
            for c in range(C):
                if c >= 2:
                    dve.wait_ge(mask_up, c - 1)
                v.tensor_scalar(under[0:N, c % 2, :, :], keys_b[0:N, :, 1:S + 1], row4[0:N, c:c + 1], None,
                                ALU.is_gt).then_inc(under_up, 1)
                if c == 0:
                    dve.wait_ge(under_up, 1)
                    v.scalar_tensor_tensor(mask[0:N, 0, :, 0:S], keys_b[0:N, :, 0:S], row4b[0:N, 0:1],
                                           under[0:N, 0, :, :], ALU.is_lt, ALU.mult).then_inc(mask_up, 1)
                if c >= 2:
                    dve.wait_ge(under_up, c)
                    v.scalar_tensor_tensor(mask[0:N, c - 1, :, 0:S], keys_b[0:N, :, 0:S], row4b[0:N, c - 1:c],
                                           under[0:N, (c - 1) % 2, :, :], ALU.is_lt, ALU.mult).then_inc(mask_up, 1)
            dve.wait_ge(under_up, C)
            v.scalar_tensor_tensor(mask[0:N, C - 1, :, 0:S], keys_b[0:N, :, 0:S], row4b[0:N, C - 1:C],
                                   under[0:N, (C - 1) % 2, :, :], ALU.is_lt, ALU.mult).then_inc(mask_up, 1)
            link(v.tensor_reduce(csum[:, :], csum_g[:, :, :], AX.X, ALU.add))
            link(v.tensor_scalar(csum[:, :], csum[:, :], 1.0 / L, None, ALU.mult))
            v.tensor_copy(csum_b[:, :, :], csum[:, :, None].to_broadcast([P, B, SP])).then_inc(csum_up, 1)
            link(v.tensor_copy(rtemp[:, :], temp_s[:, :]))
            link(v.reciprocal(rtemp[:, :], rtemp[:, :]))

            dve.wait_ge(tg_up, 2)
            for h in range(2):
                for t in (2 * h, 2 * h + 1):
                    dve.wait_ge(exp_ps, t + 1)
                    for i in range(2):
                        rows = slice(SP * i, SP * i + SP)
                        mark(v.scalar_tensor_tensor(x_s[rows, t, :], ps[rows, 1 + t, i * D:(i + 1) * D], tgx[rows, 0:1],
                                                    x_s[rows, t, :], ALU.mult, ALU.add))
                variances(h)
                normalise(2, h)
            for k in range(KS):
                dve.wait_ge(ld_ps, k + 1)
                logits = bank(XT_BANKS[2][k])[:, 0:B * S].rearrange("p (b s) -> p b s", b=B)
                link(v.reduce_max(d_max[:, k, :], logits, AX.X))
                v.tensor_tensor(disp_e[:, k, :, 0:S], logits, d_max[:, k, :, None].to_broadcast([P, B, S]),
                                ALU.subtract).then_inc(ld_sub, 1)
            for t in range(TT):
                dve.wait_ge(lc_ps, t + 1)
                v.tensor_reduce(c_nmax[:, t:t + 1], bank(1 + t), AX.X, ALU.max, negate=True).then_inc(lc_max, 1)
            for k in range(KS):
                dve.wait_ge(ld_exp, k + 1)
                mark(v.tensor_reduce(d_sum[:, k, :], disp_e[:, k, :, 0:S], AX.X, ALU.add))
            dve.wait_ge(dve_c, done[0])
            v.reciprocal(d_inv[:, :, :], d_sum[:, :, :]).then_inc(d_inv_up, 1)
            for k in range(KS):
                dve.wait_ge(comb_ps, k + 1)
                v.tensor_copy(comb_t[:, k, :], bank(1 + k)).then_inc(comb_up, 1)
            dve.wait_ge(lc_exp, TT)
            link(v.reciprocal(c_inv[:, :], c_sum[:, :]))
            link(v.tensor_scalar(tgr[:, :], c_inv[:, :], tgf[:, 0:1], None, ALU.mult))

            def add_soft(t):
                dve.wait_ge(f0_ps, t + 1)
                v.scalar_tensor_tensor(x_s[:, t, :], bank(2 + t % 2)[:, 0:D], tgr[:, t:t + 1], x_s[:, t, :],
                                       ALU.mult, ALU.add).then_inc(f0_used, 1)
                dve.wait_ge(f0_used, t + 1)

            for b in range(B):
                t, h = divmod(b, 2)
                dve.wait_ge(hy_used, 2 * (KS * (t + 1) - 1) + h + 1)
                v.tensor_copy(y_t[:, :, SP * b:SP * b + S],
                              bank(b % 2)[:, 0:Q * S].rearrange("p (q s) -> p q s", q=Q)).then_inc(y_up, 1)
                if b >= 2 and b % 2 == 0:
                    add_soft(b // 2 - 1)
                if b == 4:
                    variances(0)
            normalise(3, 0)
            add_soft(TT - 1)
            variances(1)
            normalise(3, 1)
            for h in range(2):
                for t in (2 * h, 2 * h + 1):
                    dve.wait_ge(xa_ps, t + 1)
                    mark(v.scalar_tensor_tensor(x_s[:, t, :], bank(4 + t)[:, 0:D], tgx[:, 1:2], x_s[:, t, :],
                                                ALU.mult, ALU.add))
                variances(h)
            normalise(4, 0)
            normalise(4, 1)
            dve.wait_ge(g_ps, 1)
            link(v.tensor_tensor(gates[:, :, :], bank(6)[:, 0:TT * E].rearrange("p (t e) -> p t e", e=E),
                                 gb_b[:, None, :].to_broadcast([P, TT, E]), ALU.add))
            link(v.tensor_scalar(gates[:, :, :], gates[:, :, :], rtemp[:, 0:1], None, ALU.mult))
            for t in range(TT):
                mark(v.max(top[:, t, :], gates[:, t, :]))
            dve.wait_ge(dve_c, done[0])
            v.tensor_tensor(gdiff[:, :], top[:, :, 1], top[:, :, 0], ALU.subtract).then_inc(gd_up, 1)
            for t in range(TT):
                mark(v.max_index(top_i[:, t, :], top[:, t, :], gates[:, t, :]))
            dve.wait_ge(dve_c, done[0])
            mark(v.tensor_copy(top_f[:, :, :], top_i[:, :, 0:2]))
            dve.wait_ge(ge_up, 1)
            link(v.tensor_scalar(gden[:, :], gexp[:, :], 1.0, None, ALU.add))
            link(v.reciprocal(wgt[:, 0, :], gden[:, :]))
            link(v.tensor_tensor(wgt[:, 1, :], wgt[:, 0, :], gexp[:, :], ALU.mult))
            for t in range(TT):
                for j, dst in ((0, wt1), (1, wt2)):
                    mark(v.tensor_scalar(dst[:, t, :], e_iota[:, :], top_f[:, t, j:j + 1], wgt[:, j, t:t + 1],
                                         ALU.is_equal, ALU.mult))
            dve.wait_ge(dve_c, done[0])
            v.tensor_tensor(wt[:, :, :], wt1[:, :, :], wt2[:, :, :], ALU.add).then_inc(wt_up, 1)
            dve.wait_ge(wtt_ps, 1)
            v.tensor_copy(wt_t[:, :], bank(7)[0:E, :]).then_inc(wtt_up, 1)
            dve.wait_ge(b2_ps, 1)
            v.tensor_copy(acc[:, :, :].rearrange("p t d -> p (t d)"), bank(3)).then_inc(acc_up, 1)
            for e in range(E - 2):
                dve.wait_ge(eo_ps, e + 1)
                for t in range(TT):
                    dve.wait_ge(acc_up, 1) if e == 0 else dve.wait_ge(eo_up, TT * (e - 1) + t + 1)
                    v.scalar_tensor_tensor(acc[:, t, :], bank(4 + e % 2)[:, t * D:(t + 1) * D], wt[:, t, e:e + 1],
                                           acc[:, t, :], ALU.mult, ALU.add).then_inc(eo_up, 1)
            dve.wait_ge(eo_up, TT * (E - 2))
            mark(v.tensor_scalar(wt_g[:, :, :], wt[:, :, E - 2:E], tgf[:, 1:2], None, ALU.mult))
            for t in range(TT):
                mark(v.scalar_tensor_tensor(x_s[:, t, :], acc[:, t, :], tgf[:, 1:2], x_s[:, t, :], ALU.mult, ALU.add))
            dve.wait_ge(dve_c, done[0])
            dve.wait_ge(eo_ps, E - 1)
            for t in range(TT):
                v.scalar_tensor_tensor(x_s[:, t, :], bank(4 + (E - 2) % 2)[:, t * D:(t + 1) * D], wt_g[:, t, 0:1],
                                       x_s[:, t, :], ALU.mult, ALU.add).then_inc(eo_up, 1)
            for t in range(TT):
                dve.wait_ge(eo_up, TT * (E - 2) + t + 1)
                dve.wait_ge(eo_ps, E + t)
                v.scalar_tensor_tensor(x_s[:, t, :], bank(LAST_BANKS[t])[:, 0:D], wt_g[:, t, 1:2], x_s[:, t, :],
                                       ALU.mult, ALU.add).then_inc(fin_up, 1)


_INS = ['x', 'ctx_1024', 'g_xattn', 'g_ffn', 'L0_ffn_gamma_x', 'L0_ffn_gamma_slot', 'L0_ffn_slot_embeds',
        'L0_ffn_w1', 'L0_ffn_w2', 'L1_xattn_W', 'L1_xattn_b', 'L1_ffn_W1', 'L1_ffn_b1', 'L1_ffn_W2', 'L1_ffn_b2',
        'L1_ffn_gate_w', 'L1_ffn_gate_b', 'L1_ffn_temperature']


def kernel(**inputs):
    import numpy as _np
    import concourse.bacc as _bacc
    from concourse import mybir as _mybir
    from concourse.bass_utils import run_bass_kernel_spmd as _run

    nc = _bacc.Bacc("TRN2", target_bir_lowering=False, num_devices=1)
    arrays, args = {}, []
    for name in _INS:
        a = _np.ascontiguousarray(inputs[name])
        if a.ndim == 0:
            a = a.reshape(1)
        arrays[f"in_{name}_dram"] = a
        args.append(nc.dram_tensor(f"in_{name}_dram", a.shape, _mybir.dt.from_np(a.dtype), kind="ExternalInput").ap())
    shape = inputs['x'].shape
    out = nc.dram_tensor("out_0_dram", tuple(shape), _mybir.dt.float32, kind="ExternalOutput").ap()
    gated_stack(nc, *args, out)
    r = _run(nc, [arrays], core_ids=[0])
    return r.results[0]["out_0_dram"]
```
